# Optimizing a Trainium2 kernel written in Bass

```python
import numpy as np
import jax
import jax.numpy as jnp

def _softmax(x, axis=-1):
    return jax.nn.softmax(x, axis=axis)

def _gelu(x):
    return jax.nn.gelu(x, approximate=True)

def _silu(x):
    return jax.nn.silu(x)

def _sigmoid(x):
    return jax.nn.sigmoid(x)

def _layernorm(x, axis=-1, eps=1e-05):
    m = jnp.mean(x, axis=axis, keepdims=True)
    v = jnp.var(x, axis=axis, keepdims=True)
    return (x - m) / jnp.sqrt(v + eps)

def _scatter_add(tgt, idx, src, axis=0):
    return tgt.at[idx].add(src)

def _segment_sum(src, seg, n):
    return jax.ops.segment_sum(src, seg, n)
kernel_name = 'mk_recurrent_d1_jaxref_r8_65c235'

def setup_inputs(seed: int=0):
    np.random.seed(seed)
    _w = jnp.asarray

    def _L0_attn_setup():
        import jax, jax.numpy as jnp
        import numpy as np
        B, S, D = (4, 512, 256)
        THETA = 10000.0
        LN_EPS = 1e-05

        def _layernorm(x, w, b):
            mu = jnp.mean(x, axis=-1, keepdims=True)
            var = jnp.mean(jnp.square(x - mu), axis=-1, keepdims=True)
            return (x - mu) * jax.lax.rsqrt(var + LN_EPS) * w + b

        def _rope_half(x):
            rot_dim = x.shape[-1] // 2
            seq = x.shape[-2]
            inv_freq = 1.0 / THETA ** (jnp.arange(0, rot_dim, 2, dtype=jnp.float32) / rot_dim)
            freqs = jnp.arange(seq, dtype=jnp.float32)[:, None] * inv_freq[None, :]
            freqs = jnp.repeat(freqs, 2, axis=-1)
            cos, sin = (jnp.cos(freqs), jnp.sin(freqs))
            xl, xr = (x[..., :rot_dim], x[..., rot_dim:])
            x1, x2 = (xl[..., 0::2], xl[..., 1::2])
            rh = jnp.stack((-x2, x1), axis=-1).reshape(xl.shape)
            return jnp.concatenate([xl * cos + rh * sin, xr], axis=-1)

        def _cos_sim(x):
            return x / jnp.linalg.norm(x, axis=-1, keepdims=True)
        key = jax.random.key(seed)
        k0, k1, k2 = jax.random.split(key, 3)
        X = jax.random.normal(k0, (B, S, D), jnp.float32)
        ln_w = jnp.ones((D,), jnp.float32)
        ln_b = jnp.zeros((D,), jnp.float32)
        W_in = jax.random.normal(k1, (D, 3 * D), jnp.float32) * D ** (-0.5)
        b_in = jnp.zeros((3 * D,), jnp.float32)
        W_out = jax.random.normal(k2, (D, D), jnp.float32) * D ** (-0.5)
        b_out = jnp.zeros((D,), jnp.float32)
        return {'X': X, 'ln_w': ln_w, 'ln_b': ln_b, 'W_in': W_in, 'b_in': b_in, 'W_out': W_out, 'b_out': b_out}
    _L0_attn_in = _L0_attn_setup()

    def _L0_ffn_setup():
        import jax, jax.numpy as jnp
        import numpy as np
        B, S, H, I, E, K = (4, 256, 256, 512, 8, 2)
        key = jax.random.key(seed)
        k1, k2, k3, k4 = jax.random.split(key, 4)
        return {'hidden_states': jax.random.normal(k1, (B, S, H), dtype=jnp.float32), 'gate_weight': jax.random.normal(k2, (E, H), dtype=jnp.float32) * 0.02, 'gate_up_proj': jax.random.normal(k3, (E, 2 * I, H), dtype=jnp.float32) * 0.02, 'down_proj': jax.random.normal(k4, (E, H, I), dtype=jnp.float32) * 0.02}
    _L0_ffn_in = _L0_ffn_setup()
    _d = {'L0_attn_X': _L0_attn_in['X'], 'L0_attn_ln_w': _L0_attn_in['ln_w'], 'L0_attn_ln_b': _L0_attn_in['ln_b'], 'L0_attn_W_in': _L0_attn_in['W_in'], 'L0_attn_b_in': _L0_attn_in['b_in'], 'L0_attn_W_out': _L0_attn_in['W_out'], 'L0_attn_b_out': _L0_attn_in['b_out'], 'L0_ffn_gate_weight': _L0_ffn_in['gate_weight'], 'L0_ffn_gate_up_proj': _L0_ffn_in['gate_up_proj'], 'L0_ffn_down_proj': _L0_ffn_in['down_proj']}
    _x0 = _d['L0_attn_X']
    _d['L0_attn_X'] = jax.random.normal(jax.random.fold_in(jax.random.key(seed), 1), (8, 256, 256), dtype=_x0.dtype)
    del _x0
    return _d

def reference(L0_attn_X, L0_attn_ln_w, L0_attn_ln_b, L0_attn_W_in, L0_attn_b_in, L0_attn_W_out, L0_attn_b_out, L0_ffn_gate_weight, L0_ffn_gate_up_proj, L0_ffn_down_proj):

    def _L0_attn_ref(X, ln_w, ln_b, W_in, b_in, W_out, b_out):
        import jax, jax.numpy as jnp
        import numpy as np
        B, S, D = (4, 512, 256)
        THETA = 10000.0
        LN_EPS = 1e-05

        def _layernorm(x, w, b):
            mu = jnp.mean(x, axis=-1, keepdims=True)
            var = jnp.mean(jnp.square(x - mu), axis=-1, keepdims=True)
            return (x - mu) * jax.lax.rsqrt(var + LN_EPS) * w + b

        def _rope_half(x):
            rot_dim = x.shape[-1] // 2
            seq = x.shape[-2]
            inv_freq = 1.0 / THETA ** (jnp.arange(0, rot_dim, 2, dtype=jnp.float32) / rot_dim)
            freqs = jnp.arange(seq, dtype=jnp.float32)[:, None] * inv_freq[None, :]
            freqs = jnp.repeat(freqs, 2, axis=-1)
            cos, sin = (jnp.cos(freqs), jnp.sin(freqs))
            xl, xr = (x[..., :rot_dim], x[..., rot_dim:])
            x1, x2 = (xl[..., 0::2], xl[..., 1::2])
            rh = jnp.stack((-x2, x1), axis=-1).reshape(xl.shape)
            return jnp.concatenate([xl * cos + rh * sin, xr], axis=-1)

        def _cos_sim(x):
            return x / jnp.linalg.norm(x, axis=-1, keepdims=True)
        h = _layernorm(X, ln_w, ln_b)
        qkv = h @ W_in + b_in
        Q, K, V = jnp.split(qkv, 3, axis=-1)
        Q = _rope_half(Q)
        K = _rope_half(K)
        A = jnp.sum(_cos_sim(K) * V, axis=-2)
        Y = A[:, None, :] * Q
        Y = Y @ W_out + b_out
        return Y + X

    def _L0_ffn_ref(hidden_states, gate_weight, gate_up_proj, down_proj):
        import jax, jax.numpy as jnp
        import numpy as np
        B, S, H, I, E, K = (4, 256, 256, 512, 8, 2)
        b, s, h = hidden_states.shape
        num_experts, top_k = (gate_weight.shape[0], K)
        x = hidden_states.reshape(-1, h)
        router_logits = x @ gate_weight.T
        probs = jax.nn.softmax(router_logits.astype(jnp.float32), axis=-1)
        top_v, top_i = jax.lax.top_k(probs, top_k)
        top_v = top_v / top_v.sum(axis=-1, keepdims=True)
        combine_w = jnp.einsum('tke,tk->te', jax.nn.one_hot(top_i, num_experts, dtype=top_v.dtype), top_v).astype(x.dtype)

        def expert_step(acc, inp):
            gu, dp, w = inp
            gate, up = jnp.split(x @ gu.T, 2, axis=-1)
            hidden = jax.nn.silu(gate) * up
            y = hidden @ dp.T
            return (acc + w[:, None] * y, None)
        out, _ = jax.lax.scan(expert_step, jnp.zeros_like(x), (gate_up_proj, down_proj, combine_w.T))
        return out.reshape(b, s, h)
    x = L0_attn_X
    xn = _layernorm(x, axis=-1)
    s = _L0_attn_ref(xn, L0_attn_ln_w, L0_attn_ln_b, L0_attn_W_in, L0_attn_b_in, L0_attn_W_out, L0_attn_b_out)
    g = _silu(_L0_ffn_ref(xn, L0_ffn_gate_weight, L0_ffn_gate_up_proj, L0_ffn_down_proj))
    x = x + s * g
    return x

_drawn_inputs = setup_inputs


def setup_inputs(seed=0):
    import zlib

    import numpy as np

    out = dict(_drawn_inputs(seed))
    spreads = {'L0_attn_ln_w': (1.0, 0.6),
     'L0_attn_ln_b': (0.0, 0.8),
     'L0_attn_b_in': (0.0, 0.8),
     'L0_attn_b_out': (0.0, 0.8)}
    factors = {'L0_attn_W_in': 4.311,
     'L0_attn_W_out': 4.17,
     'L0_ffn_gate_weight': 4.035,
     'L0_ffn_gate_up_proj': 3.507,
     'L0_ffn_down_proj': 3.516}
    for name, (base, spread) in spreads.items():
        noise = np.random.default_rng([zlib.crc32(name.encode()), seed]).standard_normal(out[name].shape)
        drawn = base * np.exp(spread * noise) if base else spread * noise
        out[name] = jnp.asarray(drawn.astype(out[name].dtype))
    for name, factor in factors.items():
        out[name] = (out[name] * factor).astype(out[name].dtype)
    return out
```

```python
from contextlib import ExitStack

import concourse.bass as bass
from concourse import mybir

P = 128
F32 = mybir.dt.float32
I32 = mybir.dt.int32
U32 = mybir.dt.uint32
ALU = mybir.AluOpType
ACT = mybir.ActivationFunctionType
AX_X = mybir.AxisListType.X

B, S, D = 8, 256, 256
NT = B * S // P
TPB = S // P
KD = D // P
E, TOPK = 8, 2
I = 512
KI = I // P
HALF = D // 2
QTR = HALF // 2
JOBS = (TOPK * NT * P + E * (P - 1)) // P
EPS = 1e-5
CREDIT = 16

C_IDENT = 0
C_UPPER = C_IDENT + P
C_COS = C_UPPER + P
C_SIN = C_COS + TPB * QTR
C_REV = C_SIN + TPB * QTR
C_CONT = C_REV + E * NT
C_GRID = C_CONT + E * NT
C_JOB = C_GRID + E * NT
C_ALL = C_JOB + JOBS * E


class Chain:

    def __init__(self, eng, sem):
        self.eng, self.sem, self.start, self.n, self.i, self.per = eng, sem, 0, 0, None, 0

    def enter(self, i, per):
        self.start, self.n, self.i, self.per = self.start + self.n, 0, i, per

    def leave(self, trips):
        assert self.n == self.per, self.n
        self.start, self.n, self.i = self.start + self.per * trips, 0, None

    def link(self, ins):
        ins.then_inc(self.sem, 1)
        self.n += 1
        at = self.start + self.n
        self.eng.wait_ge(self.sem, at if self.i is None else self.i * self.per + at)


def moe_mix_kernel(nc, x, ln_w, ln_b, w_in, b_in, w_out, b_out, w_gate, w_gu, w_dn, consts, out):
    with ExitStack() as ctx:
        def sb(name, shape, dt=F32):
            return ctx.enter_context(nc.sbuf_tensor(name, shape, dt))

        def sem(name):
            return ctx.enter_context(nc.semaphore(name))

        rows_in = nc.dram_tensor("rows_in", [JOBS * P, D], F32, kind="Internal").ap()
        rows_out = nc.dram_tensor("rows_out", [JOBS * P, D], F32, kind="Internal").ap()

        gu = sb("gu", [P, E, KD, 2 * I])
        dn = sb("dn", [P, E, KI, D])
        win = sb("win", [P, KD, 3 * D])
        wout = sb("wout", [P, KD, D])
        wgate = sb("wgate", [P, KD, E])
        brow = sb("brow", [1, 4 * D])
        lnwb = sb("lnwb", [P, 2, KD])
        cst = sb("cst", [P, C_ALL])
        ones = sb("ones", [P, P])
        ident = cst[:, C_IDENT:C_IDENT + P]
        upper = cst[:, C_UPPER:C_UPPER + P]
        xs = sb("xs", [P, NT, D])
        xn = sb("xn", [P, NT, D])
        ss = sb("ss", [P, NT, D])
        bns = sb("bns", [P, 2, NT, 6])
        mean = sb("mean", [P, 2, NT])
        dif = sb("dif", [P, 2, NT])
        var = sb("var", [P, 2, NT])
        std = sb("std", [P, 2, NT])
        rstd = sb("rstd", [P, 2, NT])
        ET = E * NT
        xcur = sb("xcur", [P, 2, D])
        xnT = sb("xnT", [P, 2, KD, P])
        pr = sb("pr", [P, ET])
        ex = sb("ex", [P, ET])
        tmp = sb("tmp", [P, ET])
        first = sb("first", [P, ET])
        second = sb("second", [P, ET])
        both = sb("both", [P, ET])
        cum = sb("cum", [P, ET])
        before = sb("before", [P, ET])
        slot = sb("slot", [P, ET])
        rt = sb("rt", [P, 8, NT])
        wts = sb("wts", [P, 2, NT])
        slots_f = sb("slots_f", [P, 2, NT])
        slots_i = sb("slots_i", [P, 2, NT], I32)
        nblk = sb("nblk", [P, E])
        blk_end = sb("blk_end", [P, E])
        blk_beg = sb("blk_beg", [P, E])
        jobf = sb("jobf", [1, JOBS])
        jobe = sb("jobe", [1, JOBS], I32)
        jobt = sb("jobt", [1, JOBS * E])
        work = sb("work", [P, 8192])

        off = [0]

        def cut(*shape):
            n = 1
            for s in shape:
                n *= s
            v = work[:, off[0]:off[0] + n]
            off[0] += n
            assert off[0] <= 8192
            names = "abcd"[:len(shape)]
            if len(shape) > 1:
                v = v.rearrange(f"p ({' '.join(names)}) -> p {' '.join(names)}", **dict(zip(names, shape)))
            return v

        h0 = cut(TPB, D)
        hT = cut(TPB, KD, P)
        qk = cut(2, TPB, 2, D)
        rc = cut(2, 2, HALF)
        rs = cut(2, 2, HALF)
        kv = cut(2, TPB, D)
        yT = cut(TPB, KD, P)
        ksq = cut(2, D)
        small = sb("small", [P, 16])
        knorm2, knorm, krec = (small[:, 4 * n:4 * n + 4].rearrange("p (a b) -> p a b", a=2) for n in range(3))
        amix = small[:, 12:16].rearrange("p (a b) -> p a b", a=2)
        off[0] = 0
        xg = cut(2, D)
        xgT = cut(2, KD, P)
        sil = cut(2, I)
        hid = cut(2, I)
        hidT = cut(2, KI, P)
        yo = cut(2, D)
        off[0] = 0
        RING = 4
        y1 = cut(RING, D)
        y2 = cut(RING, D)
        fo = cut(RING, D)
        go = cut(RING, D)
        oo = cut(RING, D)
        zeros = gu[:, E - 1, 0, 0:D]

        bank = [ctx.enter_context(nc.psum_tensor(f"bank{n}", [P, 512], F32)) for n in range(8)]

        s_x = sem("s_x"); s_cst = sem("s_cst"); s_win = sem("s_win"); s_wg = sem("s_wg")
        s_gu = sem("s_gu"); s_zero = sem("s_zero"); s_zfill = sem("s_zfill"); s_scat = sem("s_scat")
        s_xg = [sem(f"s_xg{n}") for n in range(2)]
        s_yst = [sem(f"s_yst{n}") for n in range(2)]
        s_gath = [sem(f"s_gath{n}") for n in range(RING)]
        s_ost = [sem(f"s_ost{n}") for n in range(RING)]
        s_dve = sem("s_dve"); s_act = sem("s_act")
        s_ones = sem("s_ones"); s_var = sem("s_var"); s_std = sem("s_std")
        s_xcur = sem("s_xcur"); s_xTp = sem("s_xTp"); s_xT = sem("s_xT"); s_logit = sem("s_logit")
        s_shift = sem("s_shift"); s_exp = sem("s_exp"); s_pick = sem("s_pick"); s_pos = sem("s_pos")
        s_slots = sem("s_slots"); s_jobs = sem("s_jobs")
        s_h0 = sem("s_h0"); s_hTp = sem("s_hTp"); s_hT = sem("s_hT"); s_qkv = sem("s_qkv")
        s_rot = sem("s_rot"); s_right = sem("s_right"); s_rope = sem("s_rope"); s_kn = sem("s_kn")
        s_kv = sem("s_kv"); s_mix = sem("s_mix"); s_amix = sem("s_amix"); s_qTp = sem("s_qTp")
        s_yT = sem("s_yT"); s_att = sem("s_att"); s_sum = sem("s_sum")
        s_jT = sem("s_jT"); s_jx = sem("s_jx"); s_gate = sem("s_gate"); s_up = sem("s_up")
        s_sil = sem("s_sil"); s_hid = sem("s_hid"); s_hTq = sem("s_hTq"); s_hidT = sem("s_hidT")
        s_down = sem("s_down"); s_yo = sem("s_yo")
        s_f = sem("s_f"); s_g = sem("s_g"); s_o = sem("s_o")

        def wait(eng, s, n):
            eng.wait_ge(s, n + CREDIT)

        def start_at_credit(eng, *sems):
            for s in sems:
                eng.sem_inc(s, CREDIT)

        def bc(ap, n, e=E):
            return ap.rearrange("p (a t) -> p a t", a=1).broadcast_to([P, e, n])

        block = ctx.enter_context(nc.Block())

        @block.sync
        def _(sp):
            start_at_credit(sp, *s_xg, *s_yst, *s_ost)
            sp.dma_start(xs[:, :, :], x.rearrange("(t p) d -> p t d", p=P)).then_inc(s_x, 16)
            sp.dma_start(cst[:, :], consts).then_inc(s_cst, 16)
            sp.dma_start(wgate[:, :, :], w_gate).then_inc(s_wg, 16)
            sp.wait_ge(s_zero, 1)
            sp.dma_start(rows_in.rearrange("(j p) d -> p j d", p=P),
                         zeros.rearrange("p (a d) -> p a d", a=1).broadcast_to([P, JOBS, D])
                         ).then_inc(s_zfill, 16)
            sp.dma_start(win[:, :, :], w_in).then_inc(s_win, 16)
            sp.dma_start(wout[:, :, :], w_out).then_inc(s_win, 16)
            sp.dma_start(brow[:, 0:3 * D], b_in).then_inc(s_win, 16)
            sp.dma_start(brow[:, 3 * D:4 * D], b_out).then_inc(s_win, 16)
            sp.dma_start(lnwb[:, 0, :], ln_w).then_inc(s_win, 16)
            sp.dma_start(lnwb[:, 1, :], ln_b).then_inc(s_win, 16)
            for e in range(E):
                if e == E - 1:
                    sp.wait_ge(s_zfill, 16)
                sp.dma_start(gu[:, e, :, :], w_gu[:, e, :, :]).then_inc(s_gu, 16)
                sp.dma_start(dn[:, e, :, :], w_dn[:, e, :, :]).then_inc(s_gu, 16)

            def load(j, u):
                wait(sp, s_jT, j - 1)
                sp.dma_start(xg[:, u, :], rows_in[bass.ds(j * P, P), :]).then_inc(s_xg[u], 16)

            def store(j, u):
                wait(sp, s_yo, j + 1)
                sp.dma_start(rows_out[bass.ds(j * P, P), :], yo[:, u, :]).then_inc(s_yst[u], 16)

            sp.wait_ge(s_scat, 16 * TOPK * NT)
            wait(sp, s_sum, NT)
            load(0, 0)
            load(1, 1)
            with sp.Fori(0, (JOBS - 3) // 2) as i:
                for u in range(2):
                    load(2 * i + u + 2, u)
                    store(2 * i + u, u)
            for j in range(JOBS - 3, JOBS):
                if j + 2 < JOBS:
                    load(j + 2, j % 2)
                store(j, j % 2)

            with sp.Fori(0, NT // RING) as i:
                for u in range(RING):
                    wait(sp, s_o, RING * i + u + 1)
                    sp.dma_start(out[bass.ds((RING * i + u) * P, P), :], oo[:, u, :]).then_inc(s_ost[u], 16)
            for u in range(RING):
                wait(sp, s_ost[u], 16 * (NT // RING))

        @block.gpsimd
        def _(pool):
            
            pool.memset(zeros, 0.0).then_inc(s_zero, 1)
            pool.memset(ones[:, :], 1.0).then_inc(s_ones, 1)
            pool.wait_ge(s_slots, 1)
            pool.wait_ge(s_zfill, 16)
            for t in range(NT):
                for c in range(TOPK):
                    pool.indirect_dma_start(
                        rows_in, bass.IndirectOffsetOnAxis(slots_i[:, c, t:t + 1], axis=0),
                        xn[:, t, :], None).then_inc(s_scat, 16)
            for u in range(2):
                wait(pool, s_yst[u], 16 * ((JOBS + 1 - u) // 2))
            for t in range(NT):
                u = t % RING
                wait(pool, s_f, t - RING + 1)
                for c, y in enumerate((y1, y2)):
                    pool.indirect_dma_start(
                        y[:, u, :], None,
                        rows_out, bass.IndirectOffsetOnAxis(slots_i[:, c, t:t + 1], axis=0)
                        ).then_inc(s_gath[u], 16)

        @block.scalar
        def _(act):
            chain = Chain(act, s_act)
            start_at_credit(act, s_xT, s_hT, s_right, s_kn, s_amix, s_sil, s_hidT, s_yo, s_g)
            act.wait_ge(s_var, 1)
            act.activation(std[:, 0, :], var[:, 0, :], ACT.Sqrt).then_inc(s_std, 1)
            with act.Fori(0, NT // 2) as i:
                for u in range(2):
                    wait(act, s_xTp, 2 * i + u + 1)
                    wait(act, s_logit, 2 * i + u - 1)
                    act.activation(xnT[:, u, :, :], bank[u][:, 0:D], ACT.Copy).then_inc(s_xT, 1)
            act.wait_ge(s_var, 2)
            act.activation(std[:, 1, :], var[:, 1, :], ACT.Sqrt).then_inc(s_std, 1)
            act.wait_ge(s_shift, 1)
            act.activation(ex[:, :], tmp[:, :], ACT.Exp).then_inc(s_exp, 1)
            act.wait_ge(s_win, 16 * 6)

            def stage1(b, w):
                for u in range(TPB):
                    t = TPB * b + u
                    wait(act, s_hTp, TPB * (b + 1))
                    wait(act, s_qkv, t - 1)
                    for k in range(KD):
                        ins = act.activation(hT[:, u, k, :], bank[0][:, u * D + k * P:u * D + (k + 1) * P],
                                             ACT.Identity, bias=lnwb[:, 1, k:k + 1], scale=lnwb[:, 0, k:k + 1])
                    ins.then_inc(s_hT, 1)
                for u in range(TPB):
                    t = TPB * b + u
                    wait(act, s_qkv, t + 1)
                    wait(act, s_qTp, t - 3)
                    act.activation(qk[:, w, u, :, HALF:D],
                                   bank[1 + u][:, :].rearrange("p (a d) -> p a d", a=2)[:, :, HALF:D],
                                   ACT.Copy).then_inc(s_right, 1)
                    wait(act, s_right, t + 1)
                    wait(act, s_rope, t + 1)
                    wait(act, s_mix, b - 1)
                    chain.link(act.activation(ksq[:, 0, :], qk[:, w, u, 1, :], ACT.Square,
                                              accum_out=knorm2[:, w, u:u + 1]))
                    act.activation(knorm[:, w, u:u + 1], knorm2[:, w, u:u + 1], ACT.Sqrt).then_inc(s_kn, 1)

            def stage2(b, w):
                wait(act, s_mix, b + 1)
                act.activation(amix[:, w, :], bank[4][:, 0:KD], ACT.Copy).then_inc(s_amix, 1)

            stage1(0, 0)
            with act.Fori(0, B // 2 - 1) as i:
                chain.enter(i, 2 * TPB)
                for w in range(2):
                    stage1(2 * i + 1 + w, 1 - w)
                    stage2(2 * i + w, w)
                chain.leave(B // 2 - 1)
            stage1(B - 1, 1)
            stage2(B - 2, 0)
            stage2(B - 1, 1)

            def silu(j, u):
                wait(act, s_gate, j + 1)
                wait(act, s_hid, j - 1)
                act.activation(sil[:, u, :], bank[u][:, :], ACT.Silu).then_inc(s_sil, 1)

            def result(j, u, round_):
                wait(act, s_down, j + 1)
                wait(act, s_yst[u], 16 * round_)
                act.activation(yo[:, u, :], bank[6][:, 0:D], ACT.Copy).then_inc(s_yo, 1)

            def hidden(j, u):
                wait(act, s_hTq, j + 1)
                wait(act, s_down, j - 1)
                act.activation(hidT[:, u, :, :], bank[4][:, :], ACT.Copy).then_inc(s_hidT, 1)

            wait(act, s_sum, NT)
            silu(0, 0)
            with act.Fori(0, (JOBS - 3) // 2) as i:
                for u in range(2):
                    j = 2 * i + u
                    silu(j + 1, 1 - u)
                    hidden(j, u)
                    result(j, u, i)
            for j in range(JOBS - 3, JOBS):
                if j + 1 < JOBS:
                    silu(j + 1, (j + 1) % 2)
                hidden(j, j % 2)
                result(j, j % 2, j // 2)

            with act.Fori(0, NT // RING) as i:
                for u in range(RING):
                    t = RING * i + u
                    wait(act, s_f, t + 1)
                    wait(act, s_o, t - RING + 1)
                    act.activation(go[:, u, :], fo[:, u, :], ACT.Silu).then_inc(s_g, 1)

        @block.tensor
        def _(pe):
            start_at_credit(pe, s_xTp, s_logit, s_hTp, s_qkv, s_mix, s_qTp, s_att, s_jT, s_gate, s_up,
                            s_hTq, s_down)
            pe.wait_ge(s_cst, 16)
            pe.wait_ge(s_wg, 16)
            with pe.Fori(0, NT // 2) as i:
                for u in range(2):
                    t = 2 * i + u
                    wait(pe, s_xcur, t + 1)
                    wait(pe, s_xT, t - 1)
                    for k in range(KD):
                        ins = pe.transpose(bank[u][:, k * P:(k + 1) * P], xcur[:, u, k * P:(k + 1) * P], ident)
                    ins.then_inc(s_xTp, 1)
                    wait(pe, s_xT, t + 1)
                    lg = bank[7][:, 0:ET].rearrange("p (e t) -> p e t", e=E)
                    for k in range(KD):
                        ins = pe.matmul(lg[:, :, bass.ds(t, 1)], xnT[:, u, k, :], wgate[:, k, :],
                                        start=(k == 0), stop=(k == KD - 1))
                    ins.then_inc(s_logit, 1)
            pe.wait_ge(s_pick, 1)
            pe.wait_ge(s_ones, 1)
            pe.matmul(bank[6][:, 0:ET], upper, both[:, :], start=True, stop=False)
            pe.matmul(bank[6][:, 0:ET], ones[:, :], before[:, :], start=False, stop=True)
            pe.matmul(bank[6][:, ET:ET + E], ones[:, :],
                      cum[:, :].rearrange("p (e t) -> p e t", e=E)[:, :, NT - 1],
                      start=True, stop=True).then_inc(s_pos, 1)
            pe.wait_ge(s_win, 16 * 6)

            def stage1(b, w):
                for u in range(TPB):
                    t = TPB * b + u
                    wait(pe, s_h0, t + 1)
                    wait(pe, s_hT, TPB * b)
                    for k in range(KD):
                        ins = pe.transpose(bank[0][:, u * D + k * P:u * D + (k + 1) * P],
                                           h0[:, u, k * P:(k + 1) * P], ident)
                    ins.then_inc(s_hTp, 1)
                for u in range(TPB):
                    t = TPB * b + u
                    wait(pe, s_hT, t + 1)
                    wait(pe, s_rot, t - 1)
                    wait(pe, s_kv, TPB * b)
                    qkp, vp = bank[1 + u][:, :], bank[3][:, u * D:(u + 1) * D]
                    for o, lo, hi in ((qkp, 0, 2 * D), (vp, 2 * D, 3 * D)):
                        pe.matmul(o, ones[0:1, :], brow[0:1, lo:hi], start=True, stop=False)
                        for k in range(KD):
                            ins = pe.matmul(o, hT[:, u, k, :], win[:, k, lo:hi], start=False, stop=(k == KD - 1))
                    ins.then_inc(s_qkv, 1)

            def stage2(b, w):
                wait(pe, s_kv, TPB * (b + 1))
                wait(pe, s_amix, b)
                for k in range(KD):
                    for u in range(TPB):
                        ins = pe.matmul(bank[4][:, k:k + 1], kv[:, w, u, k * P:(k + 1) * P], krec[:, w, u:u + 1],
                                        start=(u == 0), stop=(u == TPB - 1))
                ins.then_inc(s_mix, 1)
                for u in range(TPB):
                    t = TPB * b + u
                    wait(pe, s_rope, t + 1)
                    wait(pe, s_right, t + 1)
                    wait(pe, s_yT, TPB * b)
                    for k in range(KD):
                        ins = pe.transpose(bank[5][:, u * D + k * P:u * D + (k + 1) * P],
                                           qk[:, w, u, 0, k * P:(k + 1) * P], ident)
                    ins.then_inc(s_qTp, 1)
                for u in range(TPB):
                    t = TPB * b + u
                    wait(pe, s_yT, t + 1)
                    wait(pe, s_sum, TPB * b)
                    o = bank[7][:, u * D:(u + 1) * D]
                    pe.matmul(o, ones[0:1, :], brow[0:1, 3 * D:4 * D], start=True, stop=False)
                    for k in range(KD):
                        ins = pe.matmul(o, yT[:, u, k, :], wout[:, k, :], start=False, stop=(k == KD - 1))
                    ins.then_inc(s_att, 1)

            pe.wait_ge(s_slots, 1)
            stage1(0, 0)
            with pe.Fori(0, B // 2 - 1) as i:
                for w in range(2):
                    stage1(2 * i + 1 + w, 1 - w)
                    stage2(2 * i + w, w)
            stage1(B - 1, 1)
            stage2(B - 2, 0)
            stage2(B - 1, 1)

            pe.wait_ge(s_jobs, 1)
            pe.wait_ge(s_gu, 16 * 2 * E)
            wait(pe, s_sum, NT)

            def expert(j):
                return pe.value_load(jobe[0:1, bass.ds(j, 1)], min_val=0, max_val=E - 1)

            def turn(j, u, round_):
                wait(pe, s_xg[u], 16 * (round_ + 1))
                wait(pe, s_jx, j)
                for k in range(KD):
                    ins = pe.transpose(bank[5][:, k * P:(k + 1) * P], xg[:, u, k * P:(k + 1) * P], ident)
                ins.then_inc(s_jT, 1)

            def half(j, u, e, up):
                wait(pe, s_jx, j + 1)
                if up:
                    wait(pe, s_hid, j - 1)
                else:
                    wait(pe, s_sil, j - 1)
                for k in range(KD):
                    ins = pe.matmul(bank[2 * up + u][:, :], xgT[:, u, k, :],
                                    gu[:, bass.ds(e, 1), k, up * I:(up + 1) * I],
                                    start=(k == 0), stop=(k == KD - 1))
                ins.then_inc(s_up if up else s_gate, 1)

            def turn_hidden(j, u):
                wait(pe, s_hid, j + 1)
                wait(pe, s_hidT, j)
                for c in range(KI):
                    ins = pe.transpose(bank[4][:, c * P:(c + 1) * P], hid[:, u, c * P:(c + 1) * P], ident)
                ins.then_inc(s_hTq, 1)

            def down(j, u, e):
                wait(pe, s_hidT, j + 1)
                wait(pe, s_yo, j)
                for c in range(KI):
                    ins = pe.matmul(bank[6][:, 0:D], hidT[:, u, c, :], dn[:, bass.ds(e, 1), c, :],
                                    start=(c == 0), stop=(c == KI - 1))
                ins.then_inc(s_down, 1)

            turn(0, 0, 0)
            turn(1, 1, 0)
            e0 = expert(0)
            half(0, 0, e0, 0)
            half(0, 0, e0, 1)
            with pe.Fori(0, (JOBS - 3) // 2) as i:
                for u in range(2):
                    j = 2 * i + u
                    nxt = expert(j + 1)
                    half(j + 1, 1 - u, nxt, 0)
                    turn_hidden(j, u)
                    turn(j + 2, u, i + 1)
                    half(j + 1, 1 - u, nxt, 1)
                    down(j, u, expert(j))
            for j in range(JOBS - 3, JOBS):
                u = j % 2
                if j + 1 < JOBS:
                    nxt = expert(j + 1)
                    half(j + 1, 1 - u, nxt, 0)
                turn_hidden(j, u)
                if j + 2 < JOBS:
                    turn(j + 2, u, j // 2 + 1)
                if j + 1 < JOBS:
                    half(j + 1, 1 - u, nxt, 1)
                down(j, u, expert(j))

        @block.vector
        def _(dve):
            chain = Chain(dve, s_dve)
            link = chain.link
            start_at_credit(dve, s_rope, s_xcur, s_h0, s_rot, s_kv, s_yT, s_sum, s_jx, s_hid, s_f, s_o)

            def statistics(n):
                me, mo = bns[:, n, :, 1], bns[:, n, :, 4]
                link(dve.tensor_tensor(mean[:, n, :], me, mo, ALU.add))
                link(dve.tensor_tensor(dif[:, n, :], me, mo, ALU.subtract))
                link(dve.tensor_scalar(mean[:, n, :], mean[:, n, :], 0.5, None, ALU.mult))
                link(dve.scalar_tensor_tensor(dif[:, n, :], dif[:, n, :], 0.25, dif[:, n, :], ALU.mult, ALU.mult))
                link(dve.tensor_tensor(var[:, n, :], bns[:, n, :, 2], bns[:, n, :, 5], ALU.add))
                link(dve.scalar_tensor_tensor(var[:, n, :], var[:, n, :], 1.0 / D, dif[:, n, :], ALU.mult, ALU.add))
                dve.tensor_scalar(var[:, n, :], var[:, n, :], EPS, None, ALU.add).then_inc(s_var, 1)

            dve.wait_ge(s_x, 16)
            with dve.Fori(0, NT // 2) as i:
                chain.enter(i, 2)
                for u in range(2):
                    link(dve.bn_stats(bns[:, 0, bass.ds(2 * i + u, 1), :], xs[:, bass.ds(2 * i + u, 1), :]))
                chain.leave(NT // 2)
            statistics(0)
            dve.wait_ge(s_std, 1)
            link(dve.reciprocal(rstd[:, 0, :], std[:, 0, :]))
            with dve.Fori(0, NT // 2) as i:
                for u in range(2):
                    t = 2 * i + u
                    wait(dve, s_xTp, t - 1)
                    for o in (xcur[:, u:u + 1, :], xn[:, bass.ds(t, 1), :]):
                        ins = dve.tensor_scalar(o, xs[:, bass.ds(t, 1), :], mean[:, 0, bass.ds(t, 1)],
                                                rstd[:, 0, bass.ds(t, 1)], ALU.subtract, ALU.mult)
                    ins.then_inc(s_xcur, 1)
            wait(dve, s_xcur, NT)
            with dve.Fori(0, NT // 2) as i:
                chain.enter(i, 2)
                for u in range(2):
                    link(dve.bn_stats(bns[:, 1, bass.ds(2 * i + u, 1), :], xn[:, bass.ds(2 * i + u, 1), :]))
                chain.leave(NT // 2)
            statistics(1)

            et = lambda a: a.rearrange("p (e t) -> p e t", e=E)
            te = lambda a: a.rearrange("p (e t) -> p t e", e=E)
            logits = bank[7][:, 0:ET]
            top, total, rtotal, m1, m2, i1, den, rden = (rt[:, n, :] for n in range(8))
            wait(dve, s_logit, NT)
            link(dve.tensor_reduce(top, te(logits), AX_X, ALU.max))
            dve.tensor_tensor(et(tmp[:, :]), et(logits), bc(top, NT), ALU.subtract).then_inc(s_shift, 1)
            dve.wait_ge(s_exp, 1)
            link(dve.tensor_reduce(total, te(ex[:, :]), AX_X, ALU.add))
            link(dve.reciprocal(rtotal, total))
            link(dve.tensor_tensor(et(pr[:, :]), et(ex[:, :]), bc(rtotal, NT), ALU.mult))
            rev = cst[:, C_REV:C_REV + ET]
            dve.wait_ge(s_cst, 16)
            for m, pick in ((m1, first), (m2, second)):
                link(dve.tensor_reduce(m, te(pr[:, :]), AX_X, ALU.max))
                link(dve.tensor_tensor(et(tmp[:, :]), et(pr[:, :]), bc(m, NT), ALU.is_equal))
                link(dve.tensor_tensor(tmp[:, :], tmp[:, :], rev, ALU.mult))
                link(dve.tensor_reduce(i1, te(tmp[:, :]), AX_X, ALU.max))
                link(dve.tensor_tensor(et(pick[:, :]), et(rev), bc(i1, NT), ALU.is_equal))
                if pick is first:
                    link(dve.scalar_tensor_tensor(pr[:, :], first[:, :], -2.0, pr[:, :], ALU.mult, ALU.add))
            link(dve.tensor_tensor(both[:, :], first[:, :], second[:, :], ALU.add))
            link(dve.tensor_tensor_scan(cum[:, :], cst[:, C_CONT:C_CONT + ET], both[:, :], 0.0, ALU.mult, ALU.add))
            dve.tensor_tensor(before[:, :], cum[:, :], both[:, :], ALU.subtract).then_inc(s_pick, 1)
            link(dve.tensor_tensor(den, m1, m2, ALU.add))
            link(dve.reciprocal(rden, den))
            for c, m in enumerate((m1, m2)):
                link(dve.tensor_tensor(wts[:, c, :], m, rden, ALU.mult))
            dve.wait_ge(s_pos, 1)
            count = bank[6][:, ET:ET + E]
            link(dve.tensor_tensor(et(tmp[:, :]), count.rearrange("p (e a) -> p e a", a=1).broadcast_to([P, E, NT]),
                                   et(cst[:, C_GRID:C_GRID + ET]), ALU.is_gt))
            link(dve.tensor_reduce(nblk[:, :], et(tmp[:, :]), AX_X, ALU.add))
            link(dve.tensor_tensor_scan(blk_end[:, :], ones[:, 0:E], nblk[:, :], 0.0, ALU.mult, ALU.add))
            link(dve.tensor_tensor(blk_beg[:, :], blk_end[:, :], nblk[:, :], ALU.subtract))
            link(dve.tensor_scalar(blk_beg[:, :], blk_beg[:, :], float(P), None, ALU.mult))
            link(dve.tensor_tensor(et(slot[:, :]), et(bank[6][:, 0:ET]),
                                   blk_beg[:, :].rearrange("p (e a) -> p e a", a=1).broadcast_to([P, E, NT]), ALU.add))
            for c, pick in enumerate((first, second)):
                link(dve.tensor_tensor(tmp[:, :], slot[:, :], pick[:, :], ALU.mult))
                link(dve.tensor_reduce(slots_f[:, c, :], te(tmp[:, :]), AX_X, ALU.add))
            dve.tensor_copy(slots_i[:, :, :], slots_f[:, :, :]).then_inc(s_slots, 1)
            jt = jobt[:, :].rearrange("p (j e) -> p j e", e=E)
            link(dve.tensor_tensor(jt, cst[0:1, C_JOB:C_JOB + JOBS * E].rearrange("p (j e) -> p j e", e=E),
                                   blk_end[0:1, :].rearrange("p (a e) -> p a e", a=1).broadcast_to([1, JOBS, E]),
                                   ALU.is_ge))
            link(dve.tensor_reduce(jobf[:, :], jt, AX_X, ALU.add))
            dve.tensor_scalar(jobe[:, :], jobf[:, :], float(E - 1), None, ALU.min).then_inc(s_jobs, 1)
            dve.wait_ge(s_std, 2)
            link(dve.reciprocal(rstd[:, 1, :], std[:, 1, :]))

            def normalise(b):
                for u in range(TPB):
                    t = TPB * b + u
                    wait(dve, s_hTp, t - 1)
                    dve.tensor_scalar(h0[:, u:u + 1, :], xn[:, bass.ds(t, 1), :], mean[:, 1, bass.ds(t, 1)],
                                      rstd[:, 1, bass.ds(t, 1)], ALU.subtract, ALU.mult).then_inc(s_h0, 1)

            def stage1(b, w, last=False):
                for u in range(TPB):
                    t = TPB * b + u
                    wait(dve, s_qkv, t + 1)
                    wait(dve, s_right, t + 1)
                    ab = bank[1 + u][:, :].rearrange("p (a d) -> p a d", a=2)
                    for o, c in ((rc, C_COS), (rs, C_SIN)):
                        tab = cst[:, c + u * QTR:c + (u + 1) * QTR].rearrange("p (a b f) -> p a b f", a=1, b=1)
                        ins = dve.tensor_tensor(
                            o[:, u, :, :].rearrange("p a (b f) -> p a b f", b=2),
                            ab[:, :, 0:HALF].rearrange("p a (b f) -> p a b f", b=2),
                            tab.broadcast_to([P, 2, 2, QTR]), ALU.mult)
                    ins.then_inc(s_rot, 1)
                    wait(dve, s_rot, t + 1)
                    wait(dve, s_qTp, t - 3)
                    dve.tensor_tensor(qk[:, w, u, :, 0:QTR], rc[:, u, :, 0:QTR], rs[:, u, :, QTR:HALF], ALU.subtract)
                    dve.tensor_tensor(qk[:, w, u, :, QTR:HALF], rc[:, u, :, QTR:HALF], rs[:, u, :, 0:QTR],
                                      ALU.add).then_inc(s_rope, 1)
                if not last:
                    normalise(b + 1)
                for u in range(TPB):
                    t = TPB * b + u
                    wait(dve, s_rope, t + 1)
                    wait(dve, s_qkv, TPB * (b + 1))
                    wait(dve, s_mix, b - 1)
                    dve.tensor_tensor(kv[:, w, u, :], bank[3][:, u * D:(u + 1) * D], qk[:, w, u, 1, :], ALU.mult)
                    wait(dve, s_kn, t + 1)
                    dve.reciprocal(krec[:, w, u:u + 1], knorm[:, w, u:u + 1]).then_inc(s_kv, 1)

            def stage2(b, w):
                wait(dve, s_amix, b + 1)
                for u in range(TPB):
                    t = TPB * b + u
                    wait(dve, s_qTp, TPB * (b + 1))
                    wait(dve, s_att, t - 1)
                    for k in range(KD):
                        ins = dve.tensor_scalar(yT[:, u, k, :], bank[5][:, u * D + k * P:u * D + (k + 1) * P],
                                                amix[:, w, k:k + 1], None, ALU.mult)
                    ins.then_inc(s_yT, 1)
                for u in range(TPB):
                    t = TPB * b + u
                    wait(dve, s_att, TPB * (b + 1))
                    dve.tensor_tensor(ss[:, bass.ds(t, 1), :], bank[7][:, u * D:(u + 1) * D],
                                      xn[:, bass.ds(t, 1), :], ALU.add).then_inc(s_sum, 1)

            normalise(0)
            stage1(0, 0)
            with dve.Fori(0, B // 2 - 1) as i:
                for w in range(2):
                    stage1(2 * i + 1 + w, 1 - w)
                    stage2(2 * i + w, w)
            stage1(B - 1, 1, last=True)
            stage2(B - 2, 0)
            stage2(B - 1, 1)

            def turned(j, u):
                wait(dve, s_jT, j + 1)
                wait(dve, s_up, j - 1)
                dve.tensor_copy(xgT[:, u, :, :], bank[5][:, 0:D]).then_inc(s_jx, 1)

            def product(j, u):
                wait(dve, s_up, j + 1)
                wait(dve, s_sil, j + 1)
                wait(dve, s_hTq, j - 1)
                dve.tensor_tensor(hid[:, u, :], bank[2 + u][:, :], sil[:, u, :], ALU.mult).then_inc(s_hid, 1)

            turned(0, 0)
            turned(1, 1)
            product(0, 0)
            with dve.Fori(0, (JOBS - 3) // 2) as i:
                for u in range(2):
                    turned(2 * i + u + 2, u)
                    product(2 * i + u + 1, 1 - u)
            for j in range(JOBS - 3, JOBS - 1):
                if j + 2 < JOBS:
                    turned(j + 2, j % 2)
                product(j + 1, (j + 1) % 2)

            def mixture(t, u, round_):
                dve.wait_ge(s_gath[u], 2 * 16 * (round_ + 1))
                wait(dve, s_g, t - RING + 1)
                link(dve.tensor_scalar(fo[:, u, :], y1[:, u, :], wts[:, 0, bass.ds(t, 1)], None, ALU.mult))
                dve.scalar_tensor_tensor(fo[:, u, :], y2[:, u, :], wts[:, 1, bass.ds(t, 1)], fo[:, u, :],
                                         ALU.mult, ALU.add).then_inc(s_f, 1)

            with dve.Fori(0, NT // RING) as i:
                chain.enter(i, 2 * RING)
                for u in range(RING):
                    mixture(RING * i + u, u, i)
                for u in range(RING):
                    t = RING * i + u
                    wait(dve, s_g, t + 1)
                    wait(dve, s_ost[u], 16 * i)
                    link(dve.tensor_tensor(oo[:, u, :], ss[:, bass.ds(t, 1), :], go[:, u, :], ALU.mult))
                    dve.tensor_tensor(oo[:, u, :], xs[:, bass.ds(t, 1), :], oo[:, u, :], ALU.add).then_inc(s_o, 1)
                chain.leave(NT // RING)


def _constants():
    import numpy as np
    c = np.zeros((P, C_ALL), np.float32)
    c[:, C_IDENT:C_IDENT + P] = np.eye(P)
    c[:, C_UPPER:C_UPPER + P] = np.triu(np.ones((P, P)), 1)
    inv = (1.0 / np.float32(10000.0) ** (np.arange(0, HALF, 2, dtype=np.float32) / np.float32(HALF))).astype(np.float32)
    ang = (np.arange(S, dtype=np.float32)[:, None] * inv[None, :]).astype(np.float32)
    for at, f in ((C_COS, np.cos), (C_SIN, np.sin)):
        c[:, at:at + TPB * QTR] = f(ang).reshape(TPB, P, QTR).transpose(1, 0, 2).reshape(P, -1)
    c[:, C_REV:C_REV + E * NT] = np.repeat(E - np.arange(E), NT)
    c[:, C_CONT:C_CONT + E * NT] = np.tile((np.arange(NT) > 0), E)
    c[:, C_GRID:C_GRID + E * NT] = np.tile(P * np.arange(NT), E)
    c[:, C_JOB:C_JOB + JOBS * E] = np.repeat(np.arange(JOBS), E)
    return c


def kernel(**inputs):
    import numpy as np
    import concourse.bacc as bacc
    from concourse.bass_utils import run_bass_kernel_spmd

    a = {k: np.asarray(v) for k, v in inputs.items()}
    perm = np.concatenate([np.arange(0, HALF, 2), np.arange(1, HALF, 2), np.arange(HALF, D)])

    def chunks(w):
        return w.reshape(-1, P, w.shape[-1]).transpose(1, 0, 2)

    w_in = a["L0_attn_W_in"].reshape(D, 3, D)[:, :, perm].reshape(D, 3 * D)
    host = {
        "x": a["L0_attn_X"].reshape(B * S, D),
        "ln_w": a["L0_attn_ln_w"].reshape(KD, P).T,
        "ln_b": a["L0_attn_ln_b"].reshape(KD, P).T,
        "w_in": chunks(w_in),
        "b_in": a["L0_attn_b_in"].reshape(3, D)[:, perm].reshape(1, 3 * D),
        "w_out": chunks(a["L0_attn_W_out"][perm, :]),
        "b_out": a["L0_attn_b_out"].reshape(1, D),
        "w_gate": chunks(a["L0_ffn_gate_weight"].T),
        "w_gu": a["L0_ffn_gate_up_proj"].transpose(0, 2, 1).reshape(E, KD, P, 2 * I).transpose(2, 0, 1, 3),
        "w_dn": a["L0_ffn_down_proj"].transpose(0, 2, 1).reshape(E, KI, P, D).transpose(2, 0, 1, 3),
        "consts": _constants(),
    }
    nc = bacc.Bacc("TRN2", target_bir_lowering=False, num_devices=1)
    arrays, args = {}, []
    for name, v in host.items():
        v = np.ascontiguousarray(v)
        arrays[f"in_{name}"] = v
        args.append(nc.dram_tensor(f"in_{name}", v.shape, mybir.dt.from_np(v.dtype), kind="ExternalInput").ap())
    args.append(nc.dram_tensor("result", (B * S, D), F32, kind="ExternalOutput").ap())
    moe_mix_kernel(nc, *args)
    r = run_bass_kernel_spmd(nc, [arrays], core_ids=[0])
    return r.results[0]["result"].reshape(B, S, D)
```

```python
from contextlib import ExitStack

import concourse.bass as bass
from concourse import mybir

P = 128
F32 = mybir.dt.float32
F32R = mybir.dt.float32r
I32 = mybir.dt.int32
ALU = mybir.AluOpType
ACT = mybir.ActivationFunctionType
AX_X = mybir.AxisListType.X

B, S, D = 8, 256, 256
NT = B * S // P
TPB = S // P
KD = D // P
E, TOPK = 8, 2
I = 512
KI = I // P
HALF = D // 2
QTR = HALF // 2
JOBS = (TOPK * NT * P + E * (P - 1)) // P
EPS = 1e-5
WORK = 4608
CREDIT = 16

C_IDENT = 0
C_UPPER = C_IDENT + P
C_COS = C_UPPER + P
C_SIN = C_COS + TPB * QTR
C_REV = C_SIN + TPB * QTR
C_CONT = C_REV + E * NT
C_GRID = C_CONT + E * NT
C_JOB = C_GRID + E * NT
C_ROW = C_JOB + JOBS * E
C_ALL = C_ROW + 2


class Chain:

    def __init__(self, eng, sem):
        self.eng, self.sem, self.start, self.n, self.i, self.per = eng, sem, 0, 0, None, 0

    def enter(self, i, per):
        self.start, self.n, self.i, self.per = self.start + self.n, 0, i, per

    def leave(self, trips):
        assert self.n == self.per, self.n
        self.start, self.n, self.i = self.start + self.per * trips, 0, None

    def link(self, ins):
        ins.then_inc(self.sem, 1)
        self.n += 1
        at = self.start + self.n
        self.eng.wait_ge(self.sem, at if self.i is None else self.i * self.per + at)


def moe_mix_kernel(nc, x, ln_w, ln_b, w_in, b_in, w_out, b_out, w_gate, w_gu, w_dn, consts, out):
    with ExitStack() as ctx:
        def sb(name, shape, dt=F32):
            return ctx.enter_context(nc.sbuf_tensor(name, shape, dt))

        def sem(name):
            return ctx.enter_context(nc.semaphore(name))

        rows_in = nc.dram_tensor("rows_in", [JOBS * P, D], F32, kind="Internal").ap()
        rows_out = nc.dram_tensor("rows_out", [JOBS * P, D], F32, kind="Internal").ap()

        gu = sb("gu", [P, E, KD, 2 * I])
        dn = sb("dn", [P, E, KI, D])
        win_h, win_l = (sb(n, [P, KD, 3 * D], F32R) for n in ("win_h", "win_l"))
        wout_h, wout_l = (sb(n, [P, KD, D], F32R) for n in ("wout_h", "wout_l"))
        wgate = sb("wgate", [P, KD, E])
        bias = sb("bias", [2, 4 * D], F32R)
        ones2 = sb("ones2", [2, P], F32R)
        lnwb = sb("lnwb", [P, 2, KD])
        lnb2 = sb("lnb2", [P, KD, 2])
        cst = sb("cst", [P, C_ALL])
        ones = sb("ones", [P, P])
        ident = cst[:, C_IDENT:C_IDENT + P]
        upper = cst[:, C_UPPER:C_UPPER + P]
        xs = sb("xs", [P, NT, D])
        xn = sb("xn", [P, NT, D])
        ss = xs
        bns = sb("bns", [P, 2, NT, 6])
        mean = sb("mean", [P, 2, NT])
        dif = sb("dif", [P, 2, NT])
        var = sb("var", [P, 2, NT])
        std = sb("std", [P, 2, NT])
        rstd = sb("rstd", [P, 2, NT])
        ET = E * NT
        xcur = sb("xcur", [P, 2, D])
        xnT = sb("xnT", [P, 2, KD, P])
        pr = sb("pr", [P, ET])
        ex = sb("ex", [P, ET])
        tmp = sb("tmp", [P, ET])
        first = sb("first", [P, ET])
        second = sb("second", [P, ET])
        both = sb("both", [P, ET])
        cum = sb("cum", [P, ET])
        before = sb("before", [P, ET])
        slot = sb("slot", [P, ET])
        rt = sb("rt", [P, 8, NT])
        wts = sb("wts", [P, 2, NT])
        slots_f = sb("slots_f", [P, 2, NT])
        slots_i = sb("slots_i", [P, 2, NT], I32)
        nblk = sb("nblk", [P, E])
        blk_end = sb("blk_end", [P, E])
        blk_beg = sb("blk_beg", [P, E])
        jobf = sb("jobf", [1, JOBS])
        jobe = sb("jobe", [1, JOBS], I32)
        jobt = sb("jobt", [1, JOBS * E])
        work = sb("work", [P, WORK])
        parts = sb("parts", [P, 3072], F32R)

        off = [0]

        def cut(*shape):
            n = 1
            for s in shape:
                n *= s
            v = work[:, off[0]:off[0] + n]
            off[0] += n
            assert off[0] <= WORK
            names = "abcd"[:len(shape)]
            if len(shape) > 1:
                v = v.rearrange(f"p ({' '.join(names)}) -> p {' '.join(names)}", **dict(zip(names, shape)))
            return v

        win = cut(KD, 3 * D)
        wout = cut(KD, D)
        brow = cut(4 * D)[0:2, :]
        bias_h = cut(4 * D)[0:2, :]
        off[0] = 0
        h0 = cut(TPB, D)
        qk = cut(2, TPB, 2, D)
        rc = cut(TPB, 2, HALF)
        rs = cut(TPB, 2, HALF)
        kv = cut(TPB, D)
        ksq = cut(2, D)
        hT_h, hT_l = (parts[:, n * 1024:(n + 1) * 1024].rearrange("p (w u k q) -> p w u k q", w=2, u=TPB, k=KD)
                      for n in range(2))
        yT_h, yT_l = (parts[:, 2048 + n * 512:2048 + (n + 1) * 512].rearrange("p (u k q) -> p u k q", u=TPB, k=KD)
                      for n in range(2))
        small = sb("small", [P, 12])
        knorm2, knorm, krec = (small[:, 2 * n:2 * n + 2] for n in range(3))
        amix = small[:, 6:6 + KD]
        off[0] = 0
        xg = cut(2, D)
        xgT = cut(2, KD, P)
        sil = cut(2, I)
        hid = cut(2, I)
        hidT = cut(2, KI, P)
        yo = cut(2, D)
        off[0] = 0
        RING = 4
        y1 = cut(RING, D)
        y2 = cut(RING, D)
        fo = cut(RING, D)
        xo = cut(RING, D)
        zeros = gu[:, E - 1, 0, 0:D]

        bank = [ctx.enter_context(nc.psum_tensor(f"bank{n}", [P, 512], F32)) for n in range(8)]

        s_x = sem("s_x"); s_cst = sem("s_cst"); s_win = sem("s_win"); s_lnb = sem("s_lnb")
        s_wh = sem("s_wh"); s_wl = sem("s_wl"); s_brow = sem("s_brow"); s_bias = sem("s_bias"); s_wg = sem("s_wg")
        s_gu = sem("s_gu"); s_zero = sem("s_zero"); s_zfill = sem("s_zfill"); s_scat = sem("s_scat")
        s_xg = [sem(f"s_xg{n}") for n in range(2)]
        s_yst = [sem(f"s_yst{n}") for n in range(2)]
        s_gath = [sem(f"s_gath{n}") for n in range(RING)]
        s_xo = [sem(f"s_xo{n}") for n in range(RING)]
        s_ost = [sem(f"s_ost{n}") for n in range(RING)]
        s_dve = sem("s_dve"); s_act = sem("s_act")
        s_ones = sem("s_ones"); s_var = sem("s_var"); s_std = sem("s_std")
        s_xcur = sem("s_xcur"); s_xTp = sem("s_xTp"); s_xT = sem("s_xT"); s_logit = sem("s_logit")
        s_shift = sem("s_shift"); s_exp = sem("s_exp"); s_pick = sem("s_pick"); s_pos = sem("s_pos")
        s_slots = sem("s_slots"); s_jobs = sem("s_jobs")
        s_h0 = sem("s_h0"); s_hTp = sem("s_hTp"); s_hTh = sem("s_hTh"); s_hTl = sem("s_hTl"); s_qkv = sem("s_qkv")
        s_rot = sem("s_rot"); s_right = sem("s_right"); s_rope = sem("s_rope"); s_kn = sem("s_kn")
        s_kv = sem("s_kv"); s_mix = sem("s_mix"); s_amix = sem("s_amix"); s_qTp = sem("s_qTp")
        s_yTh = sem("s_yTh"); s_yTl = sem("s_yTl"); s_att = sem("s_att"); s_sum = sem("s_sum")
        s_jT = sem("s_jT"); s_jx = sem("s_jx"); s_gate = sem("s_gate"); s_up = sem("s_up")
        s_sil = sem("s_sil"); s_hid = sem("s_hid"); s_hTq = sem("s_hTq"); s_hidT = sem("s_hidT")
        s_down = sem("s_down"); s_yo = sem("s_yo")
        s_f = sem("s_f"); s_g = sem("s_g"); s_o = sem("s_o")

        def wait(eng, s, n):
            eng.wait_ge(s, n + CREDIT)

        def start_at_credit(eng, *sems):
            for s in sems:
                eng.sem_inc(s, CREDIT)

        def bc(ap, n, e=E):
            return ap.rearrange("p (a t) -> p a t", a=1).broadcast_to([P, e, n])

        block = ctx.enter_context(nc.Block())

        @block.sync
        def _(sp):
            start_at_credit(sp, *s_xg, *s_yst, *s_xo, *s_ost)
            sp.dma_start(xs[:, :, :], x.rearrange("(t p) d -> p t d", p=P)).then_inc(s_x, 16)
            sp.dma_start(cst[:, :], consts).then_inc(s_cst, 16)
            sp.dma_start(wgate[:, :, :], w_gate).then_inc(s_wg, 16)
            sp.dma_start(win[:, :, :], w_in).then_inc(s_win, 16)
            sp.dma_start(wout[:, :, :], w_out).then_inc(s_win, 16)
            sp.dma_start(brow[:, 0:3 * D], b_in.broadcast_to([2, 3 * D])).then_inc(s_win, 16)
            sp.dma_start(brow[:, 3 * D:4 * D], b_out.broadcast_to([2, D])).then_inc(s_win, 16)
            sp.dma_start(lnwb[:, 0, :], ln_w).then_inc(s_win, 16)
            sp.dma_start(lnwb[:, 1, :], ln_b).then_inc(s_win, 16)
            sp.wait_ge(s_zero, 1)
            sp.dma_start(rows_in.rearrange("(j p) d -> p j d", p=P),
                         zeros.rearrange("p (a d) -> p a d", a=1).broadcast_to([P, JOBS, D])
                         ).then_inc(s_zfill, 16)
            for e in range(E):
                if e == E - 1:
                    sp.wait_ge(s_zfill, 16)
                sp.dma_start(gu[:, e, :, :], w_gu[:, e, :, :]).then_inc(s_gu, 16)
                sp.dma_start(dn[:, e, :, :], w_dn[:, e, :, :]).then_inc(s_gu, 16)

            def load(j, u):
                wait(sp, s_jT, j - 1)
                sp.dma_start(xg[:, u, :], rows_in[bass.ds(j * P, P), :]).then_inc(s_xg[u], 16)

            def store(j, u):
                wait(sp, s_yo, j + 1)
                sp.dma_start(rows_out[bass.ds(j * P, P), :], yo[:, u, :]).then_inc(s_yst[u], 16)

            sp.wait_ge(s_scat, 16 * TOPK * NT)
            wait(sp, s_sum, NT)
            for j in range(4):
                load(j, j % 2)
            with sp.Fori(1, (JOBS - 3) // 2) as i:
                for u in range(2):
                    load(2 * i + u + 2, u)
                    store(2 * (i - 1) + u, u)
            load(JOBS - 1, (JOBS - 1) % 2)
            for j in range(JOBS - 5, JOBS):
                store(j, j % 2)

            def load_x(t, u, round_):
                wait(sp, s_ost[u], 16 * round_)
                sp.dma_start(xo[:, u, :], x[bass.ds(t * P, P), :]).then_inc(s_xo[u], 16)

            def store_out(t, u):
                wait(sp, s_o, t + 1)
                sp.dma_start(out[bass.ds(t * P, P), :], xo[:, u, :]).then_inc(s_ost[u], 16)

            for u in range(2):
                wait(sp, s_yst[u], 16 * ((JOBS + 1 - u) // 2))
            for u in range(RING):
                load_x(u, u, 0)
            with sp.Fori(0, NT // RING - 1) as i:
                for u in range(RING):
                    store_out(RING * i + u, u)
                for u in range(RING):
                    load_x(RING * i + u + RING, u, i + 1)
            for t in range(NT - RING, NT):
                store_out(t, t % RING)
            for u in range(RING):
                wait(sp, s_ost[u], 16 * (NT // RING))

        @block.gpsimd
        def _(pool):
            
            pool.memset(zeros, 0.0).then_inc(s_zero, 1)
            pool.memset(ones[:, :], 1.0).then_inc(s_ones, 1)
            pool.wait_ge(s_slots, 1)
            pool.wait_ge(s_zfill, 16)
            for t in range(NT):
                for c in range(TOPK):
                    pool.indirect_dma_start(
                        rows_in, bass.IndirectOffsetOnAxis(slots_i[:, c, t:t + 1], axis=0),
                        xn[:, t, :], None).then_inc(s_scat, 16)
            for u in range(2):
                wait(pool, s_yst[u], 16 * ((JOBS + 1 - u) // 2))
            for t in range(NT):
                u = t % RING
                wait(pool, s_f, t - RING + 1)
                for c, y in enumerate((y1, y2)):
                    pool.indirect_dma_start(
                        y[:, u, :], None,
                        rows_out, bass.IndirectOffsetOnAxis(slots_i[:, c, t:t + 1], axis=0)
                        ).then_inc(s_gath[u], 16)

        @block.scalar
        def _(act):
            start_at_credit(act, s_act, s_xT, s_hTh, s_right, s_kn, s_amix, s_yTh, s_sil, s_hidT, s_yo, s_g)
            act.wait_ge(s_win, 16 * 6)
            for k in range(KD):
                ins = act.activation(win_h[:, k, :], win[:, k, :], ACT.Copy, scale=lnwb[:, 0, k:k + 1])
            act.activation(wout_h[:, :, :], wout[:, :, :], ACT.Copy).then_inc(s_wh, 1)
            act.wait_ge(s_var, 1)
            act.activation(std[:, 0, :], var[:, 0, :], ACT.Sqrt).then_inc(s_std, 1)
            with act.Fori(0, NT // 2) as i:
                for u in range(2):
                    wait(act, s_xTp, 2 * i + u + 1)
                    wait(act, s_logit, 2 * i + u - 1)
                    act.activation(xnT[:, u, :, :], bank[u][:, 0:D], ACT.Copy).then_inc(s_xT, 1)
            act.wait_ge(s_var, 2)
            act.activation(std[:, 1, :], var[:, 1, :], ACT.Sqrt).then_inc(s_std, 1)
            act.wait_ge(s_shift, 1)
            act.activation(ex[:, :], tmp[:, :], ACT.Exp).then_inc(s_exp, 1)

            def copy_turned(b, w):
                wait(act, s_hTp, b + 1)
                wait(act, s_qkv, TPB * (b - 1))
                act.activation(hT_h[:, w, :, :, :], bank[0][:, :], ACT.Copy).then_inc(s_hTh, 1)

            def copy_right(b, w, u):
                wait(act, s_qkv, TPB * b + u + 1)
                wait(act, s_qTp, b - 1)
                act.activation(qk[:, w, u, :, HALF:D],
                               bank[1 + u][:, :].rearrange("p (a d) -> p a d", a=2)[:, :, HALF:D],
                               ACT.Copy).then_inc(s_right, 1)

            def mix(b):
                wait(act, s_mix, b + 1)
                act.activation(amix[:, :], bank[4][:, 0:KD], ACT.Copy).then_inc(s_amix, 1)
                wait(act, s_amix, b + 1)
                wait(act, s_qTp, b + 1)
                wait(act, s_att, TPB * b)
                for u in range(TPB):
                    for k in range(KD):
                        ins = act.activation(yT_h[:, u, k, :], bank[5][:, u * D + k * P:u * D + (k + 1) * P],
                                             ACT.Copy, scale=amix[:, k:k + 1])
                ins.then_inc(s_yTh, 1)

            def norms(b, w):
                for u in range(TPB):
                    wait(act, s_rope, TPB * b + u + 1)
                    act.activation(ksq[:, u, :], qk[:, w, u, 1, :], ACT.Square,
                                   accum_out=knorm2[:, u:u + 1]).then_inc(s_act, 1)
                wait(act, s_act, TPB * (b + 1))
                wait(act, s_kv, b)
                act.activation(knorm[:, :], knorm2[:, :], ACT.Sqrt).then_inc(s_kn, 1)

            def step(b, w, ahead=2):
                if ahead >= 1:
                    copy_right(b + 1, 1 - w, 0)
                mix(b)
                if ahead >= 2:
                    copy_turned(b + 2, w)
                if ahead >= 1:
                    copy_right(b + 1, 1 - w, 1)
                    norms(b + 1, 1 - w)

            copy_turned(0, 0)
            copy_turned(1, 1)
            for u in range(TPB):
                copy_right(0, 0, u)
            norms(0, 0)
            with act.Fori(0, B // 2 - 1) as i:
                for w in range(2):
                    step(2 * i + w, w)
            step(B - 2, 0, ahead=1)
            step(B - 1, 1, ahead=0)

            def silu(j, u):
                wait(act, s_gate, j + 1)
                wait(act, s_hid, j - 1)
                act.activation(sil[:, u, :], bank[u][:, :], ACT.Silu).then_inc(s_sil, 1)

            def result(j, u, round_):
                wait(act, s_down, j + 1)
                wait(act, s_yst[u], 16 * round_)
                act.activation(yo[:, u, :], bank[6][:, 0:D], ACT.Copy).then_inc(s_yo, 1)

            def hidden(j, u):
                wait(act, s_hTq, j + 1)
                wait(act, s_down, j - 1)
                act.activation(hidT[:, u, :, :], bank[4][:, :], ACT.Copy).then_inc(s_hidT, 1)

            wait(act, s_sum, NT)
            silu(0, 0)
            with act.Fori(0, (JOBS - 3) // 2) as i:
                for u in range(2):
                    j = 2 * i + u
                    silu(j + 1, 1 - u)
                    hidden(j, u)
                    result(j, u, i)
            for j in range(JOBS - 3, JOBS):
                if j + 1 < JOBS:
                    silu(j + 1, (j + 1) % 2)
                hidden(j, j % 2)
                result(j, j % 2, j // 2)

            with act.Fori(0, NT // RING) as i:
                for u in range(RING):
                    wait(act, s_f, RING * i + u + 1)
                    act.activation(fo[:, u, :], fo[:, u, :], ACT.Silu).then_inc(s_g, 1)

        @block.tensor
        def _(pe):
            start_at_credit(pe, s_xTp, s_logit, s_hTp, s_qkv, s_mix, s_qTp, s_att, s_jT, s_gate, s_up,
                            s_hTq, s_down)
            pe.wait_ge(s_cst, 16)
            pe.wait_ge(s_wg, 16)
            def turn_x(t, u):
                wait(pe, s_xcur, t + 1)
                wait(pe, s_xT, t - 1)
                for k in range(KD):
                    ins = pe.transpose(bank[u][:, k * P:(k + 1) * P], xcur[:, u, k * P:(k + 1) * P], ident)
                ins.then_inc(s_xTp, 1)

            def logits(t, u):
                wait(pe, s_xT, t + 1)
                lg = bank[7][:, 0:ET].rearrange("p (e t) -> p e t", e=E)
                for k in range(KD):
                    ins = pe.matmul(lg[:, :, bass.ds(t, 1)], xnT[:, u, k, :], wgate[:, k, :],
                                    start=(k == 0), stop=(k == KD - 1))
                ins.then_inc(s_logit, 1)

            turn_x(0, 0)
            with pe.Fori(0, NT // 2 - 1) as i:
                for u in range(2):
                    turn_x(2 * i + u + 1, 1 - u)
                    logits(2 * i + u, u)
            turn_x(NT - 1, 1)
            logits(NT - 2, 0)
            logits(NT - 1, 1)
            pe.wait_ge(s_lnb, 1)
            for o, lo, hi in ((bank[2], 0, 2 * D), (bank[3], 2 * D, 3 * D)):
                for k in range(KD):
                    ins = pe.matmul(o[0:2, 0:hi - lo], lnb2[:, k, :], win[:, k, lo:hi],
                                    start=(k == 0), stop=(k == KD - 1))
            ins.then_inc(s_brow, 1)
            pe.wait_ge(s_pick, 1)
            pe.wait_ge(s_ones, 1)
            pe.matmul(bank[6][:, 0:ET], upper, both[:, :], start=True, stop=False)
            pe.matmul(bank[6][:, 0:ET], ones[:, :], before[:, :], start=False, stop=True)
            pe.matmul(bank[6][:, ET:ET + E], ones[:, :],
                      cum[:, :].rearrange("p (e t) -> p e t", e=E)[:, :, NT - 1],
                      start=True, stop=True).then_inc(s_pos, 1)

            def products(o, left, right):
                for k in range(KD):
                    (lh, ll), (rh, rl) = left(k), right(k)
                    for a, c in ((lh, rh), (lh, rl), (ll, rh)):
                        ins = pe.matmul(o, a, c, start=False, stop=(k == KD - 1 and a is ll))
                return ins

            def turn_h(b):
                wait(pe, s_h0, b + 1)
                wait(pe, s_hTl, b)
                for u in range(TPB):
                    for k in range(KD):
                        ins = pe.transpose(bank[0][:, u * D + k * P:u * D + (k + 1) * P],
                                           h0[:, u, k * P:(k + 1) * P], ident)
                ins.then_inc(s_hTp, 1)

            def project(b, w, u):
                t = TPB * b + u
                if u == 0:
                    wait(pe, s_hTl, b + 1)
                    wait(pe, s_rot, TPB * b)
                    wait(pe, s_kv, b)
                for o, lo, hi in ((bank[1 + u][:, :], 0, 2 * D), (bank[3 + 3 * u][:, 0:D], 2 * D, 3 * D)):
                    pe.matmul(o, ones2[:, :], bias[:, lo:hi], start=True, stop=False)
                    ins = products(o, lambda k: (hT_h[:, w, u, k, :], hT_l[:, w, u, k, :]),
                                   lambda k: (win_h[:, k, lo:hi], win_l[:, k, lo:hi]))
                ins.then_inc(s_qkv, 1)

            def mix(b, w):
                wait(pe, s_kv, b + 1)
                wait(pe, s_amix, b)
                for k in range(KD):
                    for u in range(TPB):
                        ins = pe.matmul(bank[4][:, k:k + 1], kv[:, u, k * P:(k + 1) * P], krec[:, u:u + 1],
                                        start=(u == 0), stop=(u == TPB - 1))
                ins.then_inc(s_mix, 1)
                wait(pe, s_yTl, b)
                for u in range(TPB):
                    for k in range(KD):
                        ins = pe.transpose(bank[5][:, u * D + k * P:u * D + (k + 1) * P],
                                           qk[:, w, u, 0, k * P:(k + 1) * P], ident)
                ins.then_inc(s_qTp, 1)

            def project_out(b):
                wait(pe, s_yTl, b + 1)
                wait(pe, s_sum, TPB * b)
                for u in range(TPB):
                    o = bank[7][:, u * D:(u + 1) * D]
                    pe.matmul(o, ones2[:, :], bias[:, 3 * D:4 * D], start=True, stop=False)
                    products(o, lambda k: (yT_h[:, u, k, :], yT_l[:, u, k, :]),
                             lambda k: (wout_h[:, k, :], wout_l[:, k, :])).then_inc(s_att, 1)

            def step(b, w, ahead=2):
                if ahead >= 1:
                    project(b + 1, 1 - w, 0)
                mix(b, w)
                if ahead >= 2:
                    turn_h(b + 2)
                if ahead >= 1:
                    project(b + 1, 1 - w, 1)
                project_out(b)

            pe.wait_ge(s_slots, 1)
            pe.wait_ge(s_bias, 1)
            pe.wait_ge(s_wl, 1)
            turn_h(0)
            turn_h(1)
            for u in range(TPB):
                project(0, 0, u)
            with pe.Fori(0, B // 2 - 1) as i:
                for w in range(2):
                    step(2 * i + w, w)
            step(B - 2, 0, ahead=1)
            step(B - 1, 1, ahead=0)

            pe.wait_ge(s_jobs, 1)
            pe.wait_ge(s_gu, 16 * 2 * E)
            wait(pe, s_sum, NT)

            def expert(j):
                return pe.value_load(jobe[0:1, bass.ds(j, 1)], min_val=0, max_val=E - 1)

            def turn(j, u, round_):
                wait(pe, s_xg[u], 16 * (round_ + 1))
                wait(pe, s_jx, j)
                for k in range(KD):
                    ins = pe.transpose(bank[5][:, k * P:(k + 1) * P], xg[:, u, k * P:(k + 1) * P], ident)
                ins.then_inc(s_jT, 1)

            def half(j, u, e, up):
                wait(pe, s_jx, j + 1)
                if up:
                    wait(pe, s_hid, j - 1)
                else:
                    wait(pe, s_sil, j - 1)
                for k in range(KD):
                    ins = pe.matmul(bank[2 * up + u][:, :], xgT[:, u, k, :],
                                    gu[:, bass.ds(e, 1), k, up * I:(up + 1) * I],
                                    start=(k == 0), stop=(k == KD - 1))
                ins.then_inc(s_up if up else s_gate, 1)

            def turn_hidden(j, u):
                wait(pe, s_hid, j + 1)
                wait(pe, s_hidT, j)
                for c in range(KI):
                    ins = pe.transpose(bank[4][:, c * P:(c + 1) * P], hid[:, u, c * P:(c + 1) * P], ident)
                ins.then_inc(s_hTq, 1)

            def down(j, u, e):
                wait(pe, s_hidT, j + 1)
                wait(pe, s_yo, j)
                for c in range(KI):
                    ins = pe.matmul(bank[6][:, 0:D], hidT[:, u, c, :], dn[:, bass.ds(e, 1), c, :],
                                    start=(c == 0), stop=(c == KI - 1))
                ins.then_inc(s_down, 1)

            turn(0, 0, 0)
            turn(1, 1, 0)
            e0 = expert(0)
            half(0, 0, e0, 0)
            half(0, 0, e0, 1)
            with pe.Fori(0, (JOBS - 3) // 2) as i:
                for u in range(2):
                    j = 2 * i + u
                    nxt = expert(j + 1)
                    half(j + 1, 1 - u, nxt, 0)
                    turn_hidden(j, u)
                    turn(j + 2, u, i + 1)
                    half(j + 1, 1 - u, nxt, 1)
                    down(j, u, expert(j))
            for j in range(JOBS - 3, JOBS):
                u = j % 2
                if j + 1 < JOBS:
                    nxt = expert(j + 1)
                    half(j + 1, 1 - u, nxt, 0)
                turn_hidden(j, u)
                if j + 2 < JOBS:
                    turn(j + 2, u, j // 2 + 1)
                if j + 1 < JOBS:
                    half(j + 1, 1 - u, nxt, 1)
                down(j, u, expert(j))

        @block.vector
        def _(dve):
            chain = Chain(dve, s_dve)
            link = chain.link
            start_at_credit(dve, s_rope, s_xcur, s_h0, s_hTl, s_rot, s_kv, s_yTl, s_sum, s_jx, s_hid, s_f, s_o)

            def statistics(n):
                me, mo = bns[:, n, :, 1], bns[:, n, :, 4]
                link(dve.tensor_tensor(mean[:, n, :], me, mo, ALU.add))
                link(dve.tensor_tensor(dif[:, n, :], me, mo, ALU.subtract))
                link(dve.tensor_scalar(mean[:, n, :], mean[:, n, :], 0.5, None, ALU.mult))
                link(dve.scalar_tensor_tensor(dif[:, n, :], dif[:, n, :], 0.25, dif[:, n, :], ALU.mult, ALU.mult))
                link(dve.tensor_tensor(var[:, n, :], bns[:, n, :, 2], bns[:, n, :, 5], ALU.add))
                link(dve.scalar_tensor_tensor(var[:, n, :], var[:, n, :], 1.0 / D, dif[:, n, :], ALU.mult, ALU.add))
                dve.tensor_scalar(var[:, n, :], var[:, n, :], EPS, None, ALU.add).then_inc(s_var, 1)

            dve.memset(ones2[:, :].bitcast(F32), 1.0)
            dve.wait_ge(s_win, 16 * 6)
            dve.tensor_copy(lnb2[:, :, :], lnwb[:, 1, :].rearrange("p (k a) -> p k a", a=1).broadcast_to([P, KD, 2])
                            ).then_inc(s_lnb, 1)
            dve.wait_ge(s_x, 16)
            with dve.Fori(0, NT // 2) as i:
                chain.enter(i, 2)
                for u in range(2):
                    link(dve.bn_stats(bns[:, 0, bass.ds(2 * i + u, 1), :], xs[:, bass.ds(2 * i + u, 1), :]))
                chain.leave(NT // 2)
            statistics(0)
            dve.wait_ge(s_std, 1)
            link(dve.reciprocal(rstd[:, 0, :], std[:, 0, :]))
            with dve.Fori(0, NT // 2) as i:
                for u in range(2):
                    t = 2 * i + u
                    wait(dve, s_xTp, t - 1)
                    for o in (xcur[:, u:u + 1, :], xn[:, bass.ds(t, 1), :]):
                        ins = dve.tensor_scalar(o, xs[:, bass.ds(t, 1), :], mean[:, 0, bass.ds(t, 1)],
                                                rstd[:, 0, bass.ds(t, 1)], ALU.subtract, ALU.mult)
                    ins.then_inc(s_xcur, 1)
            wait(dve, s_xcur, NT)
            dve.wait_ge(s_wh, 1)
            for k in range(KD):
                dve.scalar_tensor_tensor(win_l[:, k, :], win[:, k, :], lnwb[:, 0, k:k + 1],
                                         win_h[:, k, :].bitcast(F32), ALU.mult, ALU.subtract)
            dve.tensor_tensor(wout_l[:, :, :], wout[:, :, :], wout_h[:, :, :].bitcast(F32),
                              ALU.subtract).then_inc(s_wl, 1)
            with dve.Fori(0, NT // 2) as i:
                chain.enter(i, 2)
                for u in range(2):
                    link(dve.bn_stats(bns[:, 1, bass.ds(2 * i + u, 1), :], xn[:, bass.ds(2 * i + u, 1), :]))
                chain.leave(NT // 2)
            statistics(1)

            dve.wait_ge(s_brow, 1)
            dve.tensor_tensor(brow[:, 0:2 * D], bank[2][0:2, :], brow[:, 0:2 * D], ALU.add)
            link(dve.tensor_tensor(brow[:, 2 * D:3 * D], bank[3][0:2, 0:D], brow[:, 2 * D:3 * D], ALU.add))
            link(dve.tensor_copy(bias[:, :], brow[:, :]))
            link(dve.tensor_scalar(bias_h[:, :], bias[:, :].bitcast(F32), cst[0:2, C_ROW:C_ROW + 1], None, ALU.mult))
            link(dve.tensor_tensor(brow[:, :], brow[:, :], bias[:, :].bitcast(F32), ALU.subtract))
            dve.scalar_tensor_tensor(bias[:, :], brow[:, :], cst[0:2, C_ROW + 1:C_ROW + 2], bias_h[:, :],
                                     ALU.mult, ALU.add).then_inc(s_bias, 1)

            et = lambda a: a.rearrange("p (e t) -> p e t", e=E)
            te = lambda a: a.rearrange("p (e t) -> p t e", e=E)
            logits = bank[7][:, 0:ET]
            top, total, rtotal, m1, m2, i1, den, rden = (rt[:, n, :] for n in range(8))
            wait(dve, s_logit, NT)
            link(dve.tensor_reduce(top, te(logits), AX_X, ALU.max))
            dve.tensor_tensor(et(tmp[:, :]), et(logits), bc(top, NT), ALU.subtract).then_inc(s_shift, 1)
            dve.wait_ge(s_exp, 1)
            link(dve.tensor_reduce(total, te(ex[:, :]), AX_X, ALU.add))
            link(dve.reciprocal(rtotal, total))
            link(dve.tensor_tensor(et(pr[:, :]), et(ex[:, :]), bc(rtotal, NT), ALU.mult))
            rev = cst[:, C_REV:C_REV + ET]
            dve.wait_ge(s_cst, 16)
            for m, pick in ((m1, first), (m2, second)):
                link(dve.tensor_reduce(m, te(pr[:, :]), AX_X, ALU.max))
                link(dve.tensor_tensor(et(tmp[:, :]), et(pr[:, :]), bc(m, NT), ALU.is_equal))
                link(dve.tensor_tensor(tmp[:, :], tmp[:, :], rev, ALU.mult))
                link(dve.tensor_reduce(i1, te(tmp[:, :]), AX_X, ALU.max))
                link(dve.tensor_tensor(et(pick[:, :]), et(rev), bc(i1, NT), ALU.is_equal))
                if pick is first:
                    link(dve.scalar_tensor_tensor(pr[:, :], first[:, :], -2.0, pr[:, :], ALU.mult, ALU.add))
            link(dve.tensor_tensor(both[:, :], first[:, :], second[:, :], ALU.add))
            link(dve.tensor_tensor_scan(cum[:, :], cst[:, C_CONT:C_CONT + ET], both[:, :], 0.0, ALU.mult, ALU.add))
            dve.tensor_tensor(before[:, :], cum[:, :], both[:, :], ALU.subtract).then_inc(s_pick, 1)
            link(dve.tensor_tensor(den, m1, m2, ALU.add))
            link(dve.reciprocal(rden, den))
            for c, m in enumerate((m1, m2)):
                link(dve.tensor_tensor(wts[:, c, :], m, rden, ALU.mult))
            dve.wait_ge(s_pos, 1)
            count = bank[6][:, ET:ET + E]
            link(dve.tensor_tensor(et(tmp[:, :]), count.rearrange("p (e a) -> p e a", a=1).broadcast_to([P, E, NT]),
                                   et(cst[:, C_GRID:C_GRID + ET]), ALU.is_gt))
            link(dve.tensor_reduce(nblk[:, :], et(tmp[:, :]), AX_X, ALU.add))
            link(dve.tensor_tensor_scan(blk_end[:, :], ones[:, 0:E], nblk[:, :], 0.0, ALU.mult, ALU.add))
            link(dve.tensor_tensor(blk_beg[:, :], blk_end[:, :], nblk[:, :], ALU.subtract))
            link(dve.tensor_scalar(blk_beg[:, :], blk_beg[:, :], float(P), None, ALU.mult))
            link(dve.tensor_tensor(et(slot[:, :]), et(bank[6][:, 0:ET]),
                                   blk_beg[:, :].rearrange("p (e a) -> p e a", a=1).broadcast_to([P, E, NT]), ALU.add))
            for c, pick in enumerate((first, second)):
                link(dve.tensor_tensor(tmp[:, :], slot[:, :], pick[:, :], ALU.mult))
                link(dve.tensor_reduce(slots_f[:, c, :], te(tmp[:, :]), AX_X, ALU.add))
            dve.tensor_copy(slots_i[:, :, :], slots_f[:, :, :]).then_inc(s_slots, 1)
            jt = jobt[:, :].rearrange("p (j e) -> p j e", e=E)
            link(dve.tensor_tensor(jt, cst[0:1, C_JOB:C_JOB + JOBS * E].rearrange("p (j e) -> p j e", e=E),
                                   blk_end[0:1, :].rearrange("p (a e) -> p a e", a=1).broadcast_to([1, JOBS, E]),
                                   ALU.is_ge))
            link(dve.tensor_reduce(jobf[:, :], jt, AX_X, ALU.add))
            dve.tensor_scalar(jobe[:, :], jobf[:, :], float(E - 1), None, ALU.min).then_inc(s_jobs, 1)
            dve.wait_ge(s_std, 2)
            link(dve.reciprocal(rstd[:, 1, :], std[:, 1, :]))

            def normalise(b):
                wait(dve, s_hTp, b)
                for u in range(TPB):
                    t = TPB * b + u
                    ins = dve.tensor_scalar(h0[:, u:u + 1, :], xn[:, bass.ds(t, 1), :], mean[:, 1, bass.ds(t, 1)],
                                            rstd[:, 1, bass.ds(t, 1)], ALU.subtract, ALU.mult)
                ins.then_inc(s_h0, 1)

            def low_turned(b, w):
                wait(dve, s_hTh, b + 1)
                dve.tensor_tensor(hT_l[:, w, :, :, :], bank[0][:, :], hT_h[:, w, :, :, :].bitcast(F32),
                                  ALU.subtract).then_inc(s_hTl, 1)

            def rotate(b, w, u):
                t = TPB * b + u
                wait(dve, s_right, t + 1)
                ab = bank[1 + u][:, :].rearrange("p (a d) -> p a d", a=2)
                for o, c in ((rc, C_COS), (rs, C_SIN)):
                    tab = cst[:, c + u * QTR:c + (u + 1) * QTR].rearrange("p (a b f) -> p a b f", a=1, b=1)
                    ins = dve.tensor_tensor(
                        o[:, u, :, :].rearrange("p a (b f) -> p a b f", b=2),
                        ab[:, :, 0:HALF].rearrange("p a (b f) -> p a b f", b=2),
                        tab.broadcast_to([P, 2, 2, QTR]), ALU.mult)
                ins.then_inc(s_rot, 1)
                wait(dve, s_rot, t + 1)
                dve.tensor_tensor(qk[:, w, u, :, 0:QTR], rc[:, u, :, 0:QTR], rs[:, u, :, QTR:HALF], ALU.subtract)
                dve.tensor_tensor(qk[:, w, u, :, QTR:HALF], rc[:, u, :, QTR:HALF], rs[:, u, :, 0:QTR],
                                  ALU.add).then_inc(s_rope, 1)

            def weigh(b, w):
                wait(dve, s_rope, TPB * (b + 1))
                wait(dve, s_mix, b)
                for u in range(TPB):
                    dve.tensor_tensor(kv[:, u, :], bank[3 + 3 * u][:, 0:D], qk[:, w, u, 1, :], ALU.mult)
                wait(dve, s_kn, b + 1)
                dve.reciprocal(krec[:, :], knorm[:, :]).then_inc(s_kv, 1)

            def low_mixed(b):
                wait(dve, s_yTh, b + 1)
                for u in range(TPB):
                    for k in range(KD):
                        ins = dve.scalar_tensor_tensor(
                            yT_l[:, u, k, :], bank[5][:, u * D + k * P:u * D + (k + 1) * P], amix[:, k:k + 1],
                            yT_h[:, u, k, :].bitcast(F32), ALU.mult, ALU.subtract)
                ins.then_inc(s_yTl, 1)

            def add_input(b):
                wait(dve, s_att, TPB * (b + 1))
                for u in range(TPB):
                    t = TPB * b + u
                    dve.tensor_tensor(ss[:, bass.ds(t, 1), :], bank[7][:, u * D:(u + 1) * D],
                                      xn[:, bass.ds(t, 1), :], ALU.add).then_inc(s_sum, 1)

            def step(b, w, ahead=3):
                if ahead >= 1:
                    rotate(b + 1, 1 - w, 0)
                low_mixed(b)
                if ahead >= 2:
                    low_turned(b + 2, w)
                if ahead >= 3:
                    normalise(b + 3)
                if ahead >= 1:
                    rotate(b + 1, 1 - w, 1)
                    weigh(b + 1, 1 - w)
                add_input(b)

            normalise(0)
            normalise(1)
            low_turned(0, 0)
            normalise(2)
            low_turned(1, 1)
            for u in range(TPB):
                rotate(0, 0, u)
            weigh(0, 0)
            with dve.Fori(0, (B - 4) // 2) as i:
                for w in range(2):
                    step(2 * i + w, w)
            for b in range(B - 4, B):
                step(b, b % 2, ahead=B - 1 - b)

            def turned(j, u):
                wait(dve, s_jT, j + 1)
                wait(dve, s_up, j - 1)
                dve.tensor_copy(xgT[:, u, :, :], bank[5][:, 0:D]).then_inc(s_jx, 1)

            def product(j, u):
                wait(dve, s_up, j + 1)
                wait(dve, s_sil, j + 1)
                wait(dve, s_hTq, j - 1)
                dve.tensor_tensor(hid[:, u, :], bank[2 + u][:, :], sil[:, u, :], ALU.mult).then_inc(s_hid, 1)

            turned(0, 0)
            turned(1, 1)
            product(0, 0)
            with dve.Fori(0, (JOBS - 3) // 2) as i:
                for u in range(2):
                    turned(2 * i + u + 2, u)
                    product(2 * i + u + 1, 1 - u)
            for j in range(JOBS - 3, JOBS - 1):
                if j + 2 < JOBS:
                    turned(j + 2, j % 2)
                product(j + 1, (j + 1) % 2)

            def mixture(t, u, round_):
                dve.wait_ge(s_gath[u], 2 * 16 * (round_ + 1))
                wait(dve, s_o, t - RING + 1)
                link(dve.tensor_scalar(fo[:, u, :], y1[:, u, :], wts[:, 0, bass.ds(t, 1)], None, ALU.mult))
                dve.scalar_tensor_tensor(fo[:, u, :], y2[:, u, :], wts[:, 1, bass.ds(t, 1)], fo[:, u, :],
                                         ALU.mult, ALU.add).then_inc(s_f, 1)

            with dve.Fori(0, NT // RING) as i:
                chain.enter(i, 2 * RING)
                for u in range(RING):
                    mixture(RING * i + u, u, i)
                for u in range(RING):
                    t = RING * i + u
                    wait(dve, s_g, t + 1)
                    link(dve.tensor_tensor(fo[:, u, :], ss[:, bass.ds(t, 1), :], fo[:, u, :], ALU.mult))
                    wait(dve, s_xo[u], 16 * (i + 1))
                    dve.tensor_tensor(xo[:, u, :], xo[:, u, :], fo[:, u, :], ALU.add).then_inc(s_o, 1)
                chain.leave(NT // RING)


def _constants():
    import numpy as np
    c = np.zeros((P, C_ALL), np.float32)
    c[:, C_IDENT:C_IDENT + P] = np.eye(P)
    c[:, C_UPPER:C_UPPER + P] = np.triu(np.ones((P, P)), 1)
    inv = (1.0 / np.float32(10000.0) ** (np.arange(0, HALF, 2, dtype=np.float32) / np.float32(HALF))).astype(np.float32)
    ang = (np.arange(S, dtype=np.float32)[:, None] * inv[None, :]).astype(np.float32)
    for at, f in ((C_COS, np.cos), (C_SIN, np.sin)):
        c[:, at:at + TPB * QTR] = f(ang).reshape(TPB, P, QTR).transpose(1, 0, 2).reshape(P, -1)
    c[:, C_REV:C_REV + E * NT] = np.repeat(E - np.arange(E), NT)
    c[:, C_CONT:C_CONT + E * NT] = np.tile((np.arange(NT) > 0), E)
    c[:, C_GRID:C_GRID + E * NT] = np.tile(P * np.arange(NT), E)
    c[:, C_JOB:C_JOB + JOBS * E] = np.repeat(np.arange(JOBS), E)
    c[0, C_ROW], c[1, C_ROW + 1] = 1, 1
    return c


def kernel(**inputs):
    import numpy as np
    import concourse.bacc as bacc
    from concourse.bass_utils import run_bass_kernel_spmd

    a = {k: np.asarray(v) for k, v in inputs.items()}
    perm = np.concatenate([np.arange(0, HALF, 2), np.arange(1, HALF, 2), np.arange(HALF, D)])

    def chunks(w):
        return w.reshape(-1, P, w.shape[-1]).transpose(1, 0, 2)

    w_in = a["L0_attn_W_in"].reshape(D, 3, D)[:, :, perm].reshape(D, 3 * D)
    host = {
        "x": a["L0_attn_X"].reshape(B * S, D),
        "ln_w": a["L0_attn_ln_w"].reshape(KD, P).T,
        "ln_b": a["L0_attn_ln_b"].reshape(KD, P).T,
        "w_in": chunks(w_in),
        "b_in": a["L0_attn_b_in"].reshape(3, D)[:, perm].reshape(1, 3 * D),
        "w_out": chunks(a["L0_attn_W_out"][perm, :]),
        "b_out": a["L0_attn_b_out"].reshape(1, D),
        "w_gate": chunks(a["L0_ffn_gate_weight"].T),
        "w_gu": a["L0_ffn_gate_up_proj"].transpose(0, 2, 1).reshape(E, KD, P, 2 * I).transpose(2, 0, 1, 3),
        "w_dn": a["L0_ffn_down_proj"].transpose(0, 2, 1).reshape(E, KI, P, D).transpose(2, 0, 1, 3),
        "consts": _constants(),
    }
    nc = bacc.Bacc("TRN2", target_bir_lowering=False, num_devices=1)
    arrays, args = {}, []
    for name, v in host.items():
        v = np.ascontiguousarray(v)
        arrays[f"in_{name}"] = v
        args.append(nc.dram_tensor(f"in_{name}", v.shape, mybir.dt.from_np(v.dtype), kind="ExternalInput").ap())
    args.append(nc.dram_tensor("result", (B * S, D), F32, kind="ExternalOutput").ap())
    moe_mix_kernel(nc, *args)
    r = run_bass_kernel_spmd(nc, [arrays], core_ids=[0])
    return r.results[0]["result"].reshape(B, S, D)
```

```python
from contextlib import ExitStack

import concourse.bass as bass
from concourse import mybir

P = 128
F32 = mybir.dt.float32
F32R = mybir.dt.float32r
I32 = mybir.dt.int32
ALU = mybir.AluOpType
ACT = mybir.ActivationFunctionType
AX_X = mybir.AxisListType.X

B, S, D = 8, 256, 256
NT = B * S // P
TPB = S // P
KD = D // P
E, TOPK = 8, 2
I = 512
KI = I // P
HALF = D // 2
QTR = HALF // 2
JOBS = (TOPK * NT * P + E * (P - 1)) // P
EPS = 1e-5
WARM = 28
FILL = 8
ROUTING_FILL = (22, 12)
XCH = 4
GRP = 2
RW = 3
NA = 4
NW = 4
CREDIT = 16

C_IDENT = 0
C_UPPER = C_IDENT + P
C_COS = C_UPPER + P
C_SIN = C_COS + TPB * QTR
C_REV = C_SIN + TPB * QTR
C_CONT = C_REV + E * NT
C_GRID = C_CONT + E * NT
C_JOB = C_GRID + E * NT
C_ROW = C_JOB + JOBS * E
C_ALL = C_ROW + 3


def chain(eng, sem):
    count = [0]

    def link(ins):
        ins.then_inc(sem, 1)
        count[0] += 1
        eng.wait_ge(sem, count[0])
    return link


def moe_mix_kernel(nc, x, ln_w, ln_b, w_in, b_in, w_out, b_out, w_gate, w_gu, w_dn, consts, out):
    with ExitStack() as ctx:
        def sb(name, shape, dt=F32):
            return ctx.enter_context(nc.sbuf_tensor(name, shape, dt))

        def sem(name):
            return ctx.enter_context(nc.semaphore(name))

        rows_in = nc.dram_tensor("rows_in", [JOBS * P, D], F32, kind="Internal").ap()
        rows_out = nc.dram_tensor("rows_out", [JOBS * P, D], F32, kind="Internal").ap()

        st_gu = sb("st_gu", [P, KD, 2 * I])
        gu_h, gu_l = (sb(n, [P, RW, KD, 2 * I], F32R) for n in ("gu_h", "gu_l"))
        dn_h, dn_l = (sb(n, [P, RW, KI, D], F32R) for n in ("dn_h", "dn_l"))
        win_h, win_l = (sb(n, [P, KD, 3 * D], F32R) for n in ("win_h", "win_l"))
        wout_h, wout_l = (sb(n, [P, KD, D], F32R) for n in ("wout_h", "wout_l"))
        wgate = sb("wgate", [P, KD, E])
        bias = sb("bias", [2, 4 * D], F32R)
        ones2 = sb("ones2", [2, P], F32R)
        lnwb = sb("lnwb", [P, 2, KD])
        lnb2 = sb("lnb2", [P, KD, 2])
        cst = sb("cst", [P, C_ALL])
        ones = sb("ones", [P, P])
        ident = cst[:, C_IDENT:C_IDENT + P]
        upper = cst[:, C_UPPER:C_UPPER + P]
        xs = sb("xs", [P, NT, D])
        xn = sb("xn", [P, NT, D])
        ss = xs
        bns = sb("bns", [P, NT, 6])
        mv = sb("mv", [P, 2, NT, 2])
        sums = sb("sums", [P, 2, NT // 2])
        dif = sb("dif", [P, NT // 2])
        eps = sb("eps", [P, 1])
        unused = sb("unused", [P, 1])
        std = sb("std", [P, 2, NT])
        rstd = sb("rstd", [P, 2, NT])
        ET = E * NT
        pr = sb("pr", [P, ET])
        ex = sb("ex", [P, ET])
        tmp = sb("tmp", [P, ET])
        first = sb("first", [P, ET])
        second = sb("second", [P, ET])
        both = sb("both", [P, ET])
        cum = sb("cum", [P, ET])
        before = ex
        slot = sb("slot", [P, ET])
        rt = sb("rt", [P, 8, NT])
        wts = sb("wts", [P, 2, NT])
        slots_f = sb("slots_f", [P, 2, NT])
        slots_i = sb("slots_i", [P, 2, NT], I32)
        nblk = sb("nblk", [P, E])
        blk_end = sb("blk_end", [P, E])
        blk_beg = sb("blk_beg", [P, E])
        blk_end_i = sb("blk_end_i", [1, E], I32)
        jobf = sb("jobf", [1, JOBS])
        jobi = sb("jobi", [1, JOBS], I32)
        jobt = sb("jobt", [1, JOBS * E])

        def cutter(tensor, size):
            at = [0]

            def cut(*shape):
                n = 1
                for d in shape:
                    n *= d
                v = tensor[:, at[0]:at[0] + n]
                at[0] += n
                assert at[0] <= size
                names = "abcd"[:len(shape)]
                if len(shape) > 1:
                    v = v.rearrange(f"p ({' '.join(names)}) -> p {' '.join(names)}", **dict(zip(names, shape)))
                return v
            return cut

        h0 = sb("h0", [P, TPB, D])
        work_a = sb("work_a", [P, 4608])
        cut = cutter(work_a, 4608)
        win = cut(KD, 3 * D)
        wout = cut(KD, D)
        brow = cut(4 * D)[0:2, :]
        winf = cut(KD, 3 * D)
        cut = cutter(work_a, 4608)
        qk = cut(2, TPB, 2, D)
        rc = cut(TPB, 2, HALF)
        rs = cut(TPB, 2, HALF)
        kv = cut(TPB, D)
        ksq = cut(2, D)
        cut = cutter(sb("parts_a", [P, 3072], F32R), 3072)
        hT_h, hT_l = (cut(2, TPB, KD, P) for n in range(2))
        yT_h, yT_l = (cut(TPB, KD, P) for n in range(2))
        small = sb("small", [P, 12])
        knorm2, knorm, krec = (small[:, 2 * n:2 * n + 2] for n in range(3))
        amix = small[:, 6:6 + KD]
        work_j = sb("work_j", [P, 4096])
        cut = cutter(work_j, 4096)
        st_dn = cut(KI, D)
        xg = cut(2, D)
        sil = cut(2, I)
        bpart = sil[0:2, :, :].rearrange("p a b -> p (a b)")
        hid = cut(2, I)
        yo = cut(2, D)
        XT = 4
        junk = xg
        xnT = hid.rearrange("p a (b k c) -> p (a b) k c", b=XT // 2, k=KD)
        zeros = yo[:, 0, :]
        cut = cutter(sb("parts_j", [P, 3072], F32R), 3072)
        xT_h, xT_l = (cut(2, KD, P) for n in range(2))
        dT_h, dT_l = (cut(2, KI, P) for n in range(2))
        x_again = work_j[:, :].rearrange("p (t d) -> p t d", t=NT)
        y1, y2 = (g[:, :, :, :].rearrange("p w k n -> p (w k n)")[:, 0:NT * D].bitcast(F32)
                  .rearrange("p (t d) -> p t d", t=NT) for g in (gu_h, gu_l))
        fo = y1

        bank = [ctx.enter_context(nc.psum_tensor(f"bank{n}", [P, 512], F32)) for n in range(8)]

        s_x = [sem(f"s_x{n}") for n in range(XCH)]
        s_ident = sem("s_ident"); s_cst = sem("s_cst"); s_wg = sem("s_wg"); s_win = sem("s_win")
        s_stgu = sem("s_stgu"); s_stdn = sem("s_stdn")
        s_xg = [sem(f"s_xg{n}") for n in range(2)]
        s_gath = [sem(f"s_gath{n}") for n in range(NT)]
        s_xa = sem("s_xa")
        s_zero = sem("s_zero"); s_zfill = sem("s_zfill"); s_scat = sem("s_scat")
        s_yst = [sem(f"s_yst{n}") for n in range(2)]
        s_ost = sem("s_ost")
        s_dve = sem("s_dve"); s_act = sem("s_act"); s_pool = sem("s_pool")
        s_wh = sem("s_wh"); s_wl = sem("s_wl"); s_ready = sem("s_ready")
        s_lnb = sem("s_lnb"); s_brow = sem("s_brow"); s_bsum = sem("s_bsum"); s_bhi = sem("s_bhi")
        s_bias = sem("s_bias")
        s_ones = sem("s_ones"); s_mv = sem("s_mv"); s_std = sem("s_std"); s_sums = sem("s_sums")
        s_xn = sem("s_xn"); s_xTp = sem("s_xTp"); s_xT = sem("s_xT"); s_logit = sem("s_logit")
        s_shift = sem("s_shift"); s_exp = sem("s_exp"); s_pick = sem("s_pick"); s_pos = sem("s_pos")
        s_slots = sem("s_slots"); s_jobs = sem("s_jobs")
        s_h0 = sem("s_h0"); s_hTp = sem("s_hTp"); s_hTh = sem("s_hTh"); s_hTl = sem("s_hTl"); s_qkv = sem("s_qkv")
        s_rot = sem("s_rot"); s_right = sem("s_right"); s_rope = sem("s_rope"); s_kn = sem("s_kn")
        s_kv = sem("s_kv"); s_mix = sem("s_mix"); s_amix = sem("s_amix"); s_qTp = sem("s_qTp")
        s_yTh = sem("s_yTh"); s_yTl = sem("s_yTl"); s_att = sem("s_att"); s_sum = sem("s_sum")
        s_jT = sem("s_jT"); s_jxh = sem("s_jxh"); s_jx = sem("s_jx"); s_gate = sem("s_gate"); s_up = sem("s_up")
        s_sil = sem("s_sil"); s_hid = sem("s_hid"); s_hTq = sem("s_hTq"); s_dTh = sem("s_dTh"); s_dT = sem("s_dT")
        s_down = sem("s_down"); s_yo = sem("s_yo")
        s_w1 = sem("s_w1"); s_f = sem("s_f"); s_g = sem("s_g"); s_o = sem("s_o"); s_o_pool = sem("s_o_pool")

        def wait(eng, s, n):
            eng.wait_ge(s, n + CREDIT)

        def start_at_credit(eng, *sems):
            for s in sems:
                eng.sem_inc(s, CREDIT)

        def bc(ap, n, e=E):
            return ap.rearrange("p (a t) -> p a t", a=1).broadcast_to([P, e, n])

        WEIGHED = {b: range(NW * (b - NA - 1), NW * (b - NA)) if b > NA else range(0) for b in range(NA, B - 1)}
        late = range(NW * (B - NA - 2), NT)

        ON_POOL = [4, 5, 6, 7]
        on_dve = [t for t in range(NT) if t not in ON_POOL]
        store_order = [0, 1, 2, 3, 8, 9, 10, 4, 11, 5, 12, 6, 13, 7, 14, 15]

        block = ctx.enter_context(nc.Block())

        @block.sync
        def _(sp):
            start_at_credit(sp, *s_xg, *s_yst)
            xch = x.rearrange("(t p) d -> p t d", p=P)

            def load_piece(n):
                tiles = slice(n * NT // XCH, (n + 1) * NT // XCH)
                sp.dma_start(xs[:, tiles, :], xch[:, tiles, :]).then_inc(s_x[n], 16)

            sp.dma_start(ident, consts[:, C_IDENT:C_IDENT + P]).then_inc(s_ident, 16)
            for n in range(XCH):
                load_piece(n)
            sp.dma_start(wgate[:, :, :], w_gate).then_inc(s_wg, 16)
            sp.dma_start(lnwb[:, 0, :], ln_w).then_inc(s_win, 16)
            sp.dma_start(lnwb[:, 1, :], ln_b).then_inc(s_win, 16)
            sp.dma_start(win[:, :, :], w_in).then_inc(s_win, 16)
            sp.dma_start(wout[:, :, :], w_out).then_inc(s_win, 16)
            sp.dma_start(brow[:, 0:3 * D], b_in.broadcast_to([2, 3 * D])).then_inc(s_win, 16)
            sp.dma_start(brow[:, 3 * D:4 * D], b_out.broadcast_to([2, D])).then_inc(s_win, 16)
            sp.dma_start(cst[:, C_UPPER:C_ALL], consts[:, C_UPPER:C_ALL]).then_inc(s_cst, 16)
            sp.wait_ge(s_zero, 1)
            sp.wait_ge(s_stgu, 16)
            sp.wait_ge(s_stdn, 16)
            sp.dma_start(rows_in.rearrange("(j p) d -> p j d", p=P),
                         zeros.rearrange("p (a d) -> p a d", a=1).broadcast_to([P, JOBS, D])
                         ).then_inc(s_zfill, 16)

            def load(j, u):
                wait(sp, s_jT, j - 1)
                sp.dma_start(xg[:, u, :], rows_in[bass.ds(j * P, P), :]).then_inc(s_xg[u], 16)

            def store(j, u):
                wait(sp, s_yo, j + 1)
                sp.dma_start(rows_out[bass.ds(j * P, P), :], yo[:, u, :]).then_inc(s_yst[u], 16)

            sp.wait_ge(s_scat, 16 * TOPK * NT)
            sp.wait_ge(s_sums, NT)
            for j in range(4):
                load(j, j % 2)
            with sp.Fori(1, (JOBS - 3) // 2) as i:
                for u in range(2):
                    load(2 * i + u + 2, u)
                    store(2 * (i - 1) + u, u)
            load(JOBS - 1, (JOBS - 1) % 2)
            for j in range(JOBS - 5, JOBS):
                store(j, j % 2)

            for u in range(2):
                wait(sp, s_yst[u], 16 * ((JOBS + 1 - u) // 2))
            sp.dma_start(x_again[:, :, :], x.rearrange("(t p) d -> p t d", p=P)).then_inc(s_xa, 16)
            for t in store_order:
                if t in ON_POOL:
                    sp.wait_ge(s_o_pool, ON_POOL.index(t) + 1)
                else:
                    sp.wait_ge(s_o, on_dve.index(t) + 1)
                sp.dma_start(out[t * P:(t + 1) * P, :], fo[:, t, :]).then_inc(s_ost, 16)
            sp.wait_ge(s_ost, 16 * NT)

        @block.gpsimd
        def _(pool):
            link = chain(pool, s_pool)
            pool.memset(eps[:, :], EPS)
            pool.memset(zeros, 0.0).then_inc(s_zero, 1)
            pool.memset(ones2[:, :].bitcast(F32), 1.0)
            pool.memset(ones[:, :], 1.0).then_inc(s_ones, 1)
            pool.wait_ge(s_ones, 1)
            pool.wait_ge(s_x[XCH - 1], 16)
            pool.dma_start(st_gu[:, :, :], w_gu[:, 0, :, :]).then_inc(s_stgu, 16)
            pool.dma_start(st_dn, w_dn[:, 0, :, :]).then_inc(s_stdn, 16)

            def high(out_, in_):
                n = in_.shape[0]
                shape = list(in_.shape)
                one = ones[0:n, 0:1]
                if len(shape) == 3:
                    one = one.rearrange("p (a b) -> p a b", a=1)
                link(pool.tensor_tensor(out_, in_, one.broadcast_to(shape), ALU.mult))

            def split_part(e, staged, s_st, hi, lo, src):
                pool.wait_ge(s_st, 16 * (e + 1))
                high(hi[:, e % RW, :, :], staged)
                link(pool.tensor_tensor(lo[:, e % RW, :, :], staged, hi[:, e % RW, :, :].bitcast(F32), ALU.subtract))
                if e + 1 < E:
                    pool.dma_start(staged, src[:, e + 1, :, :]).then_inc(s_st, 16)

            parts = ((st_gu[:, :, :], s_stgu, gu_h, gu_l, w_gu), (st_dn, s_stdn, dn_h, dn_l, w_dn))

            def split(e, between=None):
                if e >= RW:
                    pool.wait_ge(s_down, pool.value_load(blk_end_i[0:1, e - RW:e - RW + 1], min_val=0,
                                                         max_val=JOBS) + CREDIT)
                for part in parts:
                    split_part(e, *part)
                    if between is not None:
                        between()
                        between = None
                pool.sem_inc(s_ready, 1)

            def low_projections():
                pool.wait_ge(s_wh, 1)
                pool.tensor_tensor(win_l[:, :, :], winf, win_h[:, :, :].bitcast(F32), ALU.subtract)
                pool.tensor_tensor(wout_l[:, :, :], wout, wout_h[:, :, :].bitcast(F32), ALU.subtract).then_inc(s_wl, 1)

            split(0, between=low_projections)
            pool.wait_ge(s_slots, 1)
            pool.wait_ge(s_zfill, 16)
            for t in range(NT):
                for c in range(TOPK):
                    pool.indirect_dma_start(
                        rows_in, bass.IndirectOffsetOnAxis(slots_i[:, c, t:t + 1], axis=0),
                        xn[:, t, :], None).then_inc(s_scat, 16)
            pool.wait_ge(s_jobs, 1)
            for e in range(1, E):
                split(e)
            for u in range(2):
                wait(pool, s_yst[u], 16 * ((JOBS + 1 - u) // 2))
            for t in range(NT):
                for c, y in enumerate((y1, y2)):
                    pool.indirect_dma_start(
                        y[:, t, :], None, rows_out,
                        bass.IndirectOffsetOnAxis(slots_i[:, c, t:t + 1], axis=0)
                        ).then_inc(s_gath[t], 16)
            pool.wait_ge(s_xa, 16)
            for t in ON_POOL:
                wait(pool, s_g, t + 1)
                wait(pool, s_sum, t + 1)
                link(pool.tensor_tensor(fo[:, t, :], ss[:, t, :], fo[:, t, :], ALU.mult))
                pool.tensor_tensor(fo[:, t, :], x_again[:, t, :], fo[:, t, :], ALU.add
                                   ).then_inc(s_o_pool, 1)

        @block.scalar
        def _(act):
            start_at_credit(act, s_act, s_xT, s_hTh, s_right, s_kn, s_amix, s_yTh, s_sil, s_jxh, s_dTh, s_yo, s_g, s_w1)
            def deviations(n, tiles):
                act.wait_ge(s_mv, GRP * n + tiles.start // (NT // GRP) + 1)
                act.activation(std[:, n, tiles], mv[:, n, tiles, 1], ACT.Sqrt, bias=eps[:, 0:1]).then_inc(s_std, 1)

            group = [slice(n * NT // GRP, (n + 1) * NT // GRP) for n in range(GRP)]
            def sum_up(t):
                n = t - group[1].start
                for k, f in enumerate((ACT.Copy, ACT.Square)):
                    if n > 0:
                        act.wait_ge(s_sums, 2 * n + k - 1)
                    act.activation(junk[:, k, :], xn[:, t, :], f, accum_out=sums[:, k, n:n + 1]
                                   ).then_inc(s_sums, 1)

            def scaled(k):
                act.activation(winf[:, k, :], win[:, k, :], ACT.Copy, scale=lnwb[:, 0, k:k + 1])
                act.activation(win_h[:, k, :], win[:, k, :], ACT.Copy, scale=lnwb[:, 0, k:k + 1])

            act.wait_ge(s_ones, 1)
            act.activation(unused[:, :], ones[:, 0:1], ACT.Sqrt)
            deviations(0, group[0])
            for t in range(NT):
                wait(act, s_xTp, t + 1)
                if t >= XT:
                    wait(act, s_logit, t - XT + 1)
                act.activation(xnT[:, t % XT, :, :], bank[t % XT][:, 0:D], ACT.Copy).then_inc(s_xT, 1)
                if t == NT // GRP - 3:
                    deviations(0, group[1])
                if t == NT // 2 + 1:
                    act.wait_ge(s_win, 16 * 6)
                    act.activation(lnb2[:, :, :],
                                   lnwb[:, 1, :].rearrange("p (k a) -> p k a", a=1).broadcast_to([P, KD, 2]),
                                   ACT.Copy).then_inc(s_lnb, 1)
            deviations(1, group[0])
            act.wait_ge(s_shift, 1)
            act.activation(ex[:, :], tmp[:, :], ACT.Exp).then_inc(s_exp, 1)
            for k in range(KD):
                scaled(k)
            act.activation(wout_h[:, :, :], wout[:, :, :], ACT.Copy).then_inc(s_wh, 1)
            def copy_turned(b, w):
                wait(act, s_hTp, b + 1)
                wait(act, s_qkv, TPB * (b - 1))
                act.activation(hT_h[:, w, :, :, :], bank[0][:, :], ACT.Copy).then_inc(s_hTh, 1)

            def copy_right(b, w, u):
                wait(act, s_qkv, TPB * b + u + 1)
                wait(act, s_qTp, b - 1)
                act.activation(qk[:, w, u, :, HALF:D],
                               bank[1 + u][:, :].rearrange("p (a d) -> p a d", a=2)[:, :, HALF:D],
                               ACT.Copy).then_inc(s_right, 1)

            def mix(b):
                wait(act, s_mix, b + 1)
                act.activation(amix[:, :], bank[4][:, 0:KD], ACT.Copy).then_inc(s_amix, 1)
                wait(act, s_amix, b + 1)
                wait(act, s_qTp, b + 1)
                wait(act, s_att, TPB * b)
                for u in range(TPB):
                    for k in range(KD):
                        ins = act.activation(yT_h[:, u, k, :], bank[5][:, u * D + k * P:u * D + (k + 1) * P],
                                             ACT.Copy, scale=amix[:, k:k + 1])
                ins.then_inc(s_yTh, 1)

            def norms(b, w):
                for u in range(TPB):
                    wait(act, s_rope, TPB * b + u + 1)
                    act.activation(ksq[:, u, :], qk[:, w, u, 1, :], ACT.Square,
                                   accum_out=knorm2[:, u:u + 1]).then_inc(s_act, 1)
                wait(act, s_act, TPB * (b + 1))
                wait(act, s_kv, b)
                act.activation(knorm[:, :], knorm2[:, :], ACT.Sqrt).then_inc(s_kn, 1)

            def weigh_first(t):
                act.wait_ge(s_gath[t], 2 * 16)
                act.activation(fo[:, t, :], y1[:, t, :], ACT.Copy, scale=wts[:, 0, t:t + 1]
                               ).then_inc(s_w1, 1)

            def turned(j, u):
                wait(act, s_jT, j + 1)
                wait(act, s_up, j - 1)
                act.activation(xT_h[:, u, :, :], bank[5][:, 0:D], ACT.Copy).then_inc(s_jxh, 1)

            def step(b, w, ahead=2, weighed=(), into_experts=False):
                if ahead >= 1:
                    copy_right(b + 1, 1 - w, 0)
                mix(b)
                if ahead >= 2:
                    copy_turned(b + 2, w)
                if ahead >= 1:
                    copy_right(b + 1, 1 - w, 1)
                    norms(b + 1, 1 - w)
                if into_experts:
                    turned(0, 0)
                for t in weighed:
                    weigh_first(t)

            copy_turned(0, 0)
            act.wait_ge(s_bsum, 1)
            act.wait_ge(s_cst, 16)
            act.activation(bias[:, :], brow, ACT.Copy)
            act.activation(bpart, brow, ACT.Copy, scale=cst[0:2, C_ROW + 1:C_ROW + 2]).then_inc(s_bhi, 1)
            copy_turned(1, 1)
            for t in range(group[1].start, NT):
                sum_up(t)
            for u in range(TPB):
                copy_right(0, 0, u)
            norms(0, 0)
            deviations(1, group[1])
            with act.Fori(0, (NA - 1) // 2) as i:
                for w in range(2):
                    step(2 * i + w, w)
            for b in range((NA - 1) // 2 * 2, NA):
                step(b, b % 2, into_experts=b == NA - 1)

            def silu(j, u):
                wait(act, s_gate, j + 1)
                wait(act, s_hid, j - 1)
                act.activation(sil[:, u, :], bank[u][:, :], ACT.Silu).then_inc(s_sil, 1)

            def hidden(j, u):
                wait(act, s_hTq, j + 1)
                wait(act, s_down, j - 1)
                act.activation(dT_h[:, u, :, :], bank[4][:, :], ACT.Copy).then_inc(s_dTh, 1)

            def result(j, u, round_):
                wait(act, s_down, j + 1)
                wait(act, s_yst[u], 16 * round_)
                act.activation(yo[:, u, :], bank[6][:, 0:D], ACT.Copy).then_inc(s_yo, 1)

            act.wait_ge(s_zfill, 16)
            turned(1, 1)
            silu(0, 0)
            with act.Fori(0, (JOBS - 3) // 2) as i:
                for u in range(2):
                    j = 2 * i + u
                    hidden(j, u)
                    turned(j + 2, u)
                    silu(j + 1, 1 - u)
                    result(j, u, i)
            for j in range(JOBS - 3, JOBS):
                hidden(j, j % 2)
                if j + 2 < JOBS:
                    turned(j + 2, j % 2)
                if j + 1 < JOBS:
                    silu(j + 1, (j + 1) % 2)
                result(j, j % 2, j // 2)

            def gates(tiles):
                for t in tiles:
                    wait(act, s_f, t + 1)
                    act.activation(fo[:, t, :], fo[:, t, :], ACT.Silu).then_inc(s_g, 1)

            act.activation(unused[:, :], ones[:, 0:1], ACT.Sqrt)
            for b in range(NA, B - 1):
                step(b, b % 2, ahead=min(2, B - 1 - b), weighed=WEIGHED[b])
            gates(range(late.start // 2))
            step(B - 1, (B - 1) % 2, ahead=0)
            gates(range(late.start // 2, late.start))
            for t in late:
                weigh_first(t)
                if t > late.start:
                    gates([t - 1])
            gates([NT - 1])

        @block.tensor
        def _(pe):
            start_at_credit(pe, s_xTp, s_logit, s_hTp, s_qkv, s_mix, s_qTp, s_att, s_jT, s_gate, s_up,
                            s_hTq, s_down)
            pe.wait_ge(s_ones, 1)
            def keep_warm(o, n):
                for _ in range(n):
                    pe.matmul(o, ones[:, :], ones[:, :], start=True, stop=True)

            keep_warm(bank[6][:, 0:P], WARM)
            pe.wait_ge(s_ident, 16)
            pe.wait_ge(s_wg, 16)
            def turn_x(t, u):
                wait(pe, s_xn, t + 1)
                if t >= XT:
                    wait(pe, s_xT, t - XT + 1)
                for k in range(KD):
                    ins = pe.transpose(bank[u][:, k * P:(k + 1) * P], xn[:, t, k * P:(k + 1) * P], ident)
                ins.then_inc(s_xTp, 1)

            def logits(t, u):
                wait(pe, s_xT, t + 1)
                lg = bank[7][:, 0:ET].rearrange("p (e t) -> p e t", e=E)
                for k in range(KD):
                    ins = pe.matmul(lg[:, :, t], xnT[:, u, k, :], wgate[:, k, :],
                                    start=(k == 0), stop=(k == KD - 1))
                ins.then_inc(s_logit, 1)

            for t in range(XT - 2):
                turn_x(t, t)
            for t in range(NT):
                if t + XT - 2 < NT:
                    turn_x(t + XT - 2, (t + XT - 2) % XT)
                logits(t, t % XT)
                if t == NT // GRP - XT + 1:
                    keep_warm(bank[6][:, 0:P], FILL)
            pe.wait_ge(s_lnb, 1)
            for o, lo, hi in ((bank[2], 0, 2 * D), (bank[3], 2 * D, 3 * D)):
                for k in range(KD):
                    ins = pe.matmul(o[0:2, 0:hi - lo], lnb2[:, k, :], win[:, k, lo:hi],
                                    start=(k == 0), stop=(k == KD - 1))
            ins.then_inc(s_brow, 1)
            def products(o, left, right):
                for k in range(KD):
                    (lh, ll), (rh, rl) = left(k), right(k)
                    for n, (a, c) in enumerate(((lh, rh), (ll, rh), (lh, rl))):
                        pe.matmul(o, a, c, start=(k == 0 and n == 0), stop=False)

            def turn_h(b):
                wait(pe, s_h0, b + 1)
                wait(pe, s_hTl, b)
                for u in range(TPB):
                    for k in range(KD):
                        ins = pe.transpose(bank[0][:, u * D + k * P:u * D + (k + 1) * P],
                                           h0[:, u, k * P:(k + 1) * P], ident)
                ins.then_inc(s_hTp, 1)

            def project(b, w, u, first=False):
                t = TPB * b + u
                if u == 0:
                    wait(pe, s_hTl, b + 1)
                    wait(pe, s_rot, TPB * b)
                for o, lo, hi in ((bank[1 + u][:, :], 0, 2 * D), (bank[3 + 3 * u][:, 0:D], 2 * D, 3 * D)):
                    if u == 0 and lo:
                        wait(pe, s_kv, b)
                    products(o, lambda k: (hT_h[:, w, u, k, :], hT_l[:, w, u, k, :]),
                             lambda k: (win_h[:, k, lo:hi], win_l[:, k, lo:hi]))
                    if first:
                        pe.wait_ge(s_bias, 1)
                    ins = pe.matmul(o, ones2[:, :], bias[:, lo:hi], start=False, stop=True)
                ins.then_inc(s_qkv, 1)

            def mix(b, w):
                wait(pe, s_amix, b)
                wait(pe, s_kv, b + 1)
                for k in range(KD):
                    for u in range(TPB):
                        ins = pe.matmul(bank[4][:, k:k + 1], kv[:, u, k * P:(k + 1) * P], krec[:, u:u + 1],
                                        start=(u == 0), stop=(u == TPB - 1))
                ins.then_inc(s_mix, 1)
                wait(pe, s_yTl, b)
                for u in range(TPB):
                    for k in range(KD):
                        ins = pe.transpose(bank[5][:, u * D + k * P:u * D + (k + 1) * P],
                                           qk[:, w, u, 0, k * P:(k + 1) * P], ident)
                ins.then_inc(s_qTp, 1)

            def project_out(b):
                wait(pe, s_sum, TPB * b)
                wait(pe, s_yTl, b + 1)
                for u in range(TPB):
                    o = bank[7][:, u * D:(u + 1) * D]
                    products(o, lambda k: (yT_h[:, u, k, :], yT_l[:, u, k, :]),
                             lambda k: (wout_h[:, k, :], wout_l[:, k, :]))
                    pe.matmul(o, ones2[:, :], bias[:, 3 * D:4 * D], start=False, stop=True).then_inc(s_att, 1)

            def turn(j, u, round_):
                wait(pe, s_xg[u], 16 * (round_ + 1))
                wait(pe, s_jx, j)
                for k in range(KD):
                    ins = pe.transpose(bank[5][:, k * P:(k + 1) * P], xg[:, u, k * P:(k + 1) * P], ident)
                ins.then_inc(s_jT, 1)

            def step(b, w, ahead=2, into_experts=False):
                if ahead >= 1:
                    project(b + 1, 1 - w, 0)
                mix(b, w)
                if ahead >= 2:
                    turn_h(b + 2)
                if ahead >= 1:
                    project(b + 1, 1 - w, 1)
                pe.wait_ge(s_slots, 1)
                project_out(b)
                if into_experts:
                    turn(0, 0, 0)

            turn_h(0)
            keep_warm(bank[6][:, 0:P], ROUTING_FILL[0])
            turn_h(1)
            keep_warm(bank[6][:, 0:P], ROUTING_FILL[1])
            pe.wait_ge(s_pick, 1)
            pe.wait_ge(s_cst, 16)
            pe.matmul(bank[7][:, 0:ET], upper, both[:, :], start=True, stop=False)
            pe.matmul(bank[7][:, 0:ET], ones[:, :], before[:, :], start=False, stop=True)
            pe.matmul(bank[7][:, ET:ET + E], ones[:, :],
                      cum[:, :].rearrange("p (e t) -> p e t", e=E)[:, :, NT - 1],
                      start=True, stop=True).then_inc(s_pos, 1)
            pe.wait_ge(s_wl, 1)
            project(0, 0, 0, first=True)
            project(0, 0, 1)
            with pe.Fori(0, (NA - 1) // 2) as i:
                for w in range(2):
                    step(2 * i + w, w)
            for b in range((NA - 1) // 2 * 2, NA):
                step(b, b % 2, into_experts=b == NA - 1)

            pe.wait_ge(s_jobs, 1)

            def expert(j):
                return pe.value_load(jobi[0:1, bass.ds(j, 1)], min_val=0, max_val=E - 1)

            this, nxt = expert(0), expert(1)
            carried = [pe.alloc_register(f"expert{n}") for n in range(2)]
            for r, v in zip(carried, (this, nxt)):
                pe.reg_mov(r, v)

            def half(j, u, w, up):
                wait(pe, s_jx, j + 1)
                if up:
                    wait(pe, s_hid, j - 1)
                else:
                    wait(pe, s_sil, j - 1)
                n = 0
                for k in range(KD):
                    hi, lo = (g[:, bass.ds(w, 1), k, up * I:(up + 1) * I] for g in (gu_h, gu_l))
                    for a, c in ((xT_h, hi), (xT_l, hi), (xT_h, lo)):
                        ins = pe.matmul(bank[2 * up + u][:, :], a[:, u, k, :], c, start=(n == 0),
                                        stop=(n == 3 * KD - 1))
                        n += 1
                ins.then_inc(s_up if up else s_gate, 1)

            def turn_hidden(j, u):
                wait(pe, s_hid, j + 1)
                wait(pe, s_dT, j)
                for c in range(KI):
                    ins = pe.transpose(bank[4][:, c * P:(c + 1) * P], hid[:, u, c * P:(c + 1) * P], ident)
                ins.then_inc(s_hTq, 1)

            def down(j, u, w):
                wait(pe, s_dTh, j + 1)
                wait(pe, s_yo, j)
                wait(pe, s_dT, j + 1)
                n = 0
                for c in range(KI):
                    hi, lo = (g[:, bass.ds(w, 1), c, :] for g in (dn_h, dn_l))
                    for a, b_ in ((dT_h, hi), (dT_l, hi), (dT_h, lo)):
                        ins = pe.matmul(bank[6][:, 0:D], a[:, u, c, :], b_, start=(n == 0), stop=(n == 3 * KI - 1))
                        n += 1
                ins.then_inc(s_down, 1)

            def ready(e):
                pe.wait_ge(s_ready, e + 1)
                return e % RW

            def job_step(j, u, this, nxt, turned=None):
                turn_hidden(j, u)
                if turned is not None:
                    turn(j + 2, u, turned)
                if nxt is not None:
                    at = ready(nxt)
                    half(j + 1, 1 - u, at, 0)
                    half(j + 1, 1 - u, at, 1)
                after = expert(j + 2) if turned is not None else None
                down(j, u, this % RW)
                return after

            turn(1, 1, 0)
            wait(pe, s_hTl, NA + 2)
            wait(pe, s_rot, TPB * (NA + 1))
            wait(pe, s_kv, NA + 1)
            at = ready(this)
            half(0, 0, at, 0)
            half(0, 0, at, 1)

            def from_carried():
                return [pe.snap(r, min_val=0, max_val=E - 1) for r in carried]

            with pe.Fori(0, (JOBS - 3) // 2) as i:
                this, nxt = from_carried()
                for u in range(2):
                    this, nxt = nxt, job_step(2 * i + u, u, this, nxt, turned=i + 1)
                for r, v in zip(carried, (this, nxt)):
                    pe.reg_mov(r, v)
            this, nxt = from_carried()
            for j in range(JOBS - 3, JOBS):
                this, nxt = nxt, job_step(j, j % 2, this, nxt, turned=j // 2 + 1 if j + 2 < JOBS else None)

            wait(pe, s_yo, JOBS)
            for b in range(NA, B):
                step(b, b % 2, ahead=min(2, B - 1 - b))

        @block.vector
        def _(dve):
            link = chain(dve, s_dve)
            start_at_credit(dve, s_rope, s_xn, s_h0, s_hTl, s_rot, s_kv, s_yTl, s_sum, s_jx, s_hid, s_dT, s_f)

            def aggregate(n, tiles):
                for t in range(tiles.start, tiles.stop):
                    ins = dve.bn_aggr(mv[:, n, t, :], bns[:, t, :])
                ins.then_inc(s_mv, 1)

            def reciprocals(n, tiles):
                dve.wait_ge(s_std, GRP * n + tiles.start // (NT // GRP) + 1)
                link(dve.reciprocal(rstd[:, n, tiles], std[:, n, tiles]))

            def moments(n, tiles):
                for t in range(tiles.start, tiles.stop):
                    if n == 0 and t % (NT // XCH) == 0:
                        dve.wait_ge(s_x[t * XCH // NT], 16)
                    ins = dve.bn_stats(bns[:, t, :], (xs, xn)[n][:, t, :])
                link(ins)
                aggregate(n, tiles)

            group = [slice(n * NT // GRP, (n + 1) * NT // GRP) for n in range(GRP)]
            for tiles in group:
                moments(0, tiles)
                reciprocals(0, tiles)
                for t in range(tiles.start, tiles.stop):
                    dve.tensor_scalar(xn[:, t, :], xs[:, t, :], mv[:, 0, t, 0:1], rstd[:, 0, t:t + 1],
                                      ALU.subtract, ALU.mult).then_inc(s_xn, 1)
            wait(dve, s_xn, NT)
            moments(1, group[0])
            reciprocals(1, group[0])
            def normalise(b):
                wait(dve, s_hTp, b)
                for u in range(TPB):
                    t = TPB * b + u
                    ins = dve.tensor_scalar(h0[:, u:u + 1, :], xn[:, bass.ds(t, 1), :], mv[:, 1, bass.ds(t, 1), 0],
                                            rstd[:, 1, bass.ds(t, 1)], ALU.subtract, ALU.mult)
                ins.then_inc(s_h0, 1)

            def low_turned(b, w):
                wait(dve, s_hTh, b + 1)
                dve.tensor_tensor(hT_l[:, w, :, :, :], bank[0][:, :], hT_h[:, w, :, :, :].bitcast(F32),
                                  ALU.subtract).then_inc(s_hTl, 1)

            def rotate(b, w, u):
                t = TPB * b + u
                wait(dve, s_right, t + 1)
                ab = bank[1 + u][:, :].rearrange("p (a d) -> p a d", a=2)
                for o, c in ((rc, C_COS), (rs, C_SIN)):
                    tab = cst[:, c + u * QTR:c + (u + 1) * QTR].rearrange("p (a b f) -> p a b f", a=1, b=1)
                    ins = dve.tensor_tensor(
                        o[:, u, :, :].rearrange("p a (b f) -> p a b f", b=2),
                        ab[:, :, 0:HALF].rearrange("p a (b f) -> p a b f", b=2),
                        tab.broadcast_to([P, 2, 2, QTR]), ALU.mult)
                ins.then_inc(s_rot, 1)
                wait(dve, s_rot, t + 1)
                dve.tensor_tensor(qk[:, w, u, :, 0:QTR], rc[:, u, :, 0:QTR], rs[:, u, :, QTR:HALF], ALU.subtract)
                dve.tensor_tensor(qk[:, w, u, :, QTR:HALF], rc[:, u, :, QTR:HALF], rs[:, u, :, 0:QTR],
                                  ALU.add).then_inc(s_rope, 1)

            def weigh(b, w):
                wait(dve, s_rope, TPB * (b + 1))
                wait(dve, s_mix, b)
                for u in range(TPB):
                    dve.tensor_tensor(kv[:, u, :], bank[3 + 3 * u][:, 0:D], qk[:, w, u, 1, :], ALU.mult)
                wait(dve, s_kn, b + 1)
                dve.reciprocal(krec[:, :], knorm[:, :]).then_inc(s_kv, 1)

            def low_mixed(b):
                wait(dve, s_yTh, b + 1)
                for u in range(TPB):
                    for k in range(KD):
                        ins = dve.scalar_tensor_tensor(
                            yT_l[:, u, k, :], bank[5][:, u * D + k * P:u * D + (k + 1) * P], amix[:, k:k + 1],
                            yT_h[:, u, k, :].bitcast(F32), ALU.mult, ALU.subtract)
                ins.then_inc(s_yTl, 1)

            def add_input(b):
                wait(dve, s_att, TPB * (b + 1))
                for u in range(TPB):
                    t = TPB * b + u
                    dve.tensor_tensor(ss[:, bass.ds(t, 1), :], bank[7][:, u * D:(u + 1) * D],
                                      xn[:, bass.ds(t, 1), :], ALU.add).then_inc(s_sum, 1)

            def weigh_second(t):
                wait(dve, s_w1, t + 1)
                dve.scalar_tensor_tensor(fo[:, t, :], y2[:, t, :], wts[:, 1, t:t + 1],
                                         fo[:, t, :], ALU.mult, ALU.add).then_inc(s_f, 1)

            def finish(t):
                wait(dve, s_g, t + 1)
                link(dve.tensor_tensor(fo[:, t, :], ss[:, t, :], fo[:, t, :], ALU.mult))
                dve.tensor_tensor(fo[:, t, :], x_again[:, t, :], fo[:, t, :], ALU.add).then_inc(s_o, 1)

            def turned(j, u):
                wait(dve, s_jxh, j + 1)
                wait(dve, s_up, j - 1)
                dve.tensor_tensor(xT_l[:, u, :, :], bank[5][:, 0:D], xT_h[:, u, :, :].bitcast(F32),
                                  ALU.subtract).then_inc(s_jx, 1)

            def step(b, w, ahead=3, weighed=(), into_experts=False):
                if ahead >= 1:
                    rotate(b + 1, 1 - w, 0)
                low_mixed(b)
                if ahead >= 2:
                    low_turned(b + 2, w)
                if ahead >= 3:
                    normalise(b + 3)
                if ahead >= 1:
                    rotate(b + 1, 1 - w, 1)
                    weigh(b + 1, 1 - w)
                if into_experts:
                    turned(0, 0)
                for t in weighed:
                    weigh_second(t)
                add_input(b)

            et = lambda a: a.rearrange("p (e t) -> p e t", e=E)
            te = lambda a: a.rearrange("p (e t) -> p t e", e=E)
            logits = bank[7][:, 0:ET]
            top, total, rtotal, m1, m2, i1, den, rden = (rt[:, n, :] for n in range(8))
            wait(dve, s_logit, NT)
            link(dve.tensor_reduce(top, te(logits), AX_X, ALU.max))
            dve.tensor_tensor(et(tmp[:, :]), et(logits), bc(top, NT), ALU.subtract).then_inc(s_shift, 1)
            normalise(0)
            dve.wait_ge(s_exp, 1)
            link(dve.tensor_reduce(total, te(ex[:, :]), AX_X, ALU.add))
            dve.wait_ge(s_brow, 1)
            dve.wait_ge(s_win, 16 * 6)
            dve.tensor_tensor(brow[:, 0:2 * D], brow[:, 0:2 * D], bank[2][0:2, :], ALU.add)
            dve.tensor_tensor(brow[:, 2 * D:3 * D], brow[:, 2 * D:3 * D], bank[3][0:2, 0:D], ALU.add).then_inc(s_bsum, 1)
            link(dve.reciprocal(rtotal, total))
            link(dve.tensor_tensor(et(pr[:, :]), et(ex[:, :]), bc(rtotal, NT), ALU.mult))
            normalise(1)
            rev = cst[:, C_REV:C_REV + ET]
            dve.wait_ge(s_cst, 16)
            for m, pick in ((m1, first), (m2, second)):
                link(dve.tensor_reduce(m, te(pr[:, :]), AX_X, ALU.max))
                link(dve.tensor_tensor(et(tmp[:, :]), et(pr[:, :]), bc(m, NT), ALU.is_equal))
                link(dve.tensor_tensor(tmp[:, :], tmp[:, :], rev, ALU.mult))
                link(dve.tensor_reduce(i1, te(tmp[:, :]), AX_X, ALU.max))
                link(dve.tensor_tensor(et(pick[:, :]), et(rev), bc(i1, NT), ALU.is_equal))
                if pick is first:
                    link(dve.scalar_tensor_tensor(pr[:, :], first[:, :], -2.0, pr[:, :], ALU.mult, ALU.add))
                    low_turned(0, 0)
            link(dve.tensor_tensor(both[:, :], first[:, :], second[:, :], ALU.add))
            link(dve.tensor_tensor_scan(cum[:, :], cst[:, C_CONT:C_CONT + ET], both[:, :], 0.0, ALU.mult, ALU.add))
            dve.tensor_tensor(before[:, :], cum[:, :], both[:, :], ALU.subtract).then_inc(s_pick, 1)
            dve.wait_ge(s_bhi, 1)
            dve.scalar_tensor_tensor(bias[:, :], bias[:, :].bitcast(F32), cst[0:2, C_ROW + 2:C_ROW + 3], bpart,
                                     ALU.mult, ALU.add).then_inc(s_bias, 1)
            dve.wait_ge(s_pos, 1)
            count = bank[7][:, ET:ET + E]
            link(dve.tensor_tensor(et(tmp[:, :]), count.rearrange("p (e a) -> p e a", a=1).broadcast_to([P, E, NT]),
                                   et(cst[:, C_GRID:C_GRID + ET]), ALU.is_gt))
            link(dve.tensor_reduce(nblk[:, :], et(tmp[:, :]), AX_X, ALU.add))
            link(dve.tensor_tensor_scan(blk_end[:, :], ones[:, 0:E], nblk[:, :], 0.0, ALU.mult, ALU.add))
            link(dve.tensor_tensor(blk_beg[:, :], blk_end[:, :], nblk[:, :], ALU.subtract))
            link(dve.tensor_scalar(blk_beg[:, :], blk_beg[:, :], float(P), None, ALU.mult))
            link(dve.tensor_tensor(et(slot[:, :]), et(bank[7][:, 0:ET]),
                                   blk_beg[:, :].rearrange("p (e a) -> p e a", a=1).broadcast_to([P, E, NT]), ALU.add))
            for c, pick in enumerate((first, second)):
                link(dve.tensor_tensor(tmp[:, :], slot[:, :], pick[:, :], ALU.mult))
                link(dve.tensor_reduce(slots_f[:, c, :], te(tmp[:, :]), AX_X, ALU.add))
            dve.tensor_copy(slots_i[:, :, :], slots_f[:, :, :]).then_inc(s_slots, 1)
            low_turned(1, 1)
            normalise(2)
            dve.wait_ge(s_wl, 1)
            for u in range(TPB):
                rotate(0, 0, u)
            dve.wait_ge(s_slots, 1)
            link(dve.tensor_copy(blk_end_i[:, :], blk_end[0:1, :]))
            jt = jobt[:, :].rearrange("p (j e) -> p j e", e=E)
            link(dve.tensor_tensor(jt, cst[0:1, C_JOB:C_JOB + JOBS * E].rearrange("p (j e) -> p j e", e=E),
                                   blk_end[0:1, :].rearrange("p (a e) -> p a e", a=1).broadcast_to([1, JOBS, E]),
                                   ALU.is_ge))
            link(dve.tensor_reduce(jobf[:, :], jt, AX_X, ALU.add))
            dve.tensor_scalar(jobi[:, :], jobf[:, :], float(E - 1), None, ALU.min).then_inc(s_jobs, 1)
            weigh(0, 0)
            link(dve.tensor_tensor(den, m1, m2, ALU.add))
            link(dve.reciprocal(rden, den))
            for c, m in enumerate((m1, m2)):
                link(dve.tensor_tensor(wts[:, c, :], m, rden, ALU.mult))
            assert GRP == 2
            tiles = group[1]
            dve.wait_ge(s_sums, NT)
            link(dve.tensor_scalar(mv[:, 1, tiles, 0], sums[:, 0, :], 1.0 / D, None, ALU.mult))
            link(dve.tensor_tensor(dif[:, :], mv[:, 1, tiles, 0], mv[:, 1, tiles, 0], ALU.mult))
            dve.scalar_tensor_tensor(mv[:, 1, tiles, 1], sums[:, 1, :], 1.0 / D, dif[:, :], ALU.mult, ALU.subtract
                                     ).then_inc(s_mv, 1)
            reciprocals(1, tiles)
            with dve.Fori(0, (NA - 1) // 2) as i:
                for w in range(2):
                    step(2 * i + w, w)
            for b in range((NA - 1) // 2 * 2, NA):
                step(b, b % 2, into_experts=b == NA - 1)

            def product(j, u):
                wait(dve, s_up, j + 1)
                wait(dve, s_sil, j + 1)
                wait(dve, s_hTq, j - 1)
                dve.tensor_tensor(hid[:, u, :], bank[2 + u][:, :], sil[:, u, :], ALU.mult).then_inc(s_hid, 1)

            def hidden(j, u):
                wait(dve, s_dTh, j + 1)
                wait(dve, s_down, j - 1)
                dve.tensor_tensor(dT_l[:, u, :, :], bank[4][:, :], dT_h[:, u, :, :].bitcast(F32),
                                  ALU.subtract).then_inc(s_dT, 1)

            turned(1, 1)
            product(0, 0)
            with dve.Fori(0, (JOBS - 3) // 2) as i:
                for u in range(2):
                    hidden(2 * i + u, u)
                    turned(2 * i + u + 2, u)
                    product(2 * i + u + 1, 1 - u)
            for j in range(JOBS - 3, JOBS):
                hidden(j, j % 2)
                if j + 2 < JOBS:
                    turned(j + 2, j % 2)
                if j + 1 < JOBS:
                    product(j + 1, (j + 1) % 2)

            for b in range(NA, B - 1):
                step(b, b % 2, ahead=B - 1 - b, weighed=WEIGHED[b])
            dve.wait_ge(s_xa, 16)
            for t in range(late.start):
                if t == late.start // 2:
                    low_mixed(B - 1)
                if t in on_dve:
                    finish(t)
            for t in late:
                if t == TPB * (B - 1):
                    add_input(B - 1)
                weigh_second(t)
                if t - 1 in late and t - 1 in on_dve:
                    finish(t - 1)
            finish(NT - 1)


def _constants():
    import numpy as np
    c = np.zeros((P, C_ALL), np.float32)
    c[:, C_IDENT:C_IDENT + P] = np.eye(P)
    c[:, C_UPPER:C_UPPER + P] = np.triu(np.ones((P, P)), 1)
    inv = (1.0 / np.float32(10000.0) ** (np.arange(0, HALF, 2, dtype=np.float32) / np.float32(HALF))).astype(np.float32)
    ang = (np.arange(S, dtype=np.float32)[:, None] * inv[None, :]).astype(np.float32)
    for at, f in ((C_COS, np.cos), (C_SIN, np.sin)):
        c[:, at:at + TPB * QTR] = f(ang).reshape(TPB, P, QTR).transpose(1, 0, 2).reshape(P, -1)
    c[:, C_REV:C_REV + E * NT] = np.repeat(E - np.arange(E), NT)
    c[:, C_CONT:C_CONT + E * NT] = np.tile((np.arange(NT) > 0), E)
    c[:, C_GRID:C_GRID + E * NT] = np.tile(P * np.arange(NT), E)
    c[:, C_JOB:C_JOB + JOBS * E] = np.repeat(np.arange(JOBS), E)
    c[0, C_ROW], c[1, C_ROW + 1] = 1, 1
    c[0, C_ROW + 2], c[1, C_ROW + 2] = 1, -1
    return c


def kernel(**inputs):
    import numpy as np
    import concourse.bacc as bacc
    from concourse.bass_utils import run_bass_kernel_spmd

    a = {k: np.asarray(v) for k, v in inputs.items()}
    perm = np.concatenate([np.arange(0, HALF, 2), np.arange(1, HALF, 2), np.arange(HALF, D)])

    def chunks(w):
        return w.reshape(-1, P, w.shape[-1]).transpose(1, 0, 2)

    w_in = a["L0_attn_W_in"].reshape(D, 3, D)[:, :, perm].reshape(D, 3 * D)
    host = {
        "x": a["L0_attn_X"].reshape(B * S, D),
        "ln_w": a["L0_attn_ln_w"].reshape(KD, P).T,
        "ln_b": a["L0_attn_ln_b"].reshape(KD, P).T,
        "w_in": chunks(w_in),
        "b_in": a["L0_attn_b_in"].reshape(3, D)[:, perm].reshape(1, 3 * D),
        "w_out": chunks(a["L0_attn_W_out"][perm, :]),
        "b_out": a["L0_attn_b_out"].reshape(1, D),
        "w_gate": chunks(a["L0_ffn_gate_weight"].T),
        "w_gu": a["L0_ffn_gate_up_proj"].transpose(0, 2, 1).reshape(E, KD, P, 2 * I).transpose(2, 0, 1, 3),
        "w_dn": a["L0_ffn_down_proj"].transpose(0, 2, 1).reshape(E, KI, P, D).transpose(2, 0, 1, 3),
        "consts": _constants(),
    }
    nc = bacc.Bacc("TRN2", target_bir_lowering=False, num_devices=1)
    arrays, args = {}, []
    for name, v in host.items():
        v = np.ascontiguousarray(v)
        arrays[f"in_{name}"] = v
        args.append(nc.dram_tensor(f"in_{name}", v.shape, mybir.dt.from_np(v.dtype), kind="ExternalInput").ap())
    args.append(nc.dram_tensor("result", (B * S, D), F32, kind="ExternalOutput").ap())
    moe_mix_kernel(nc, *args)
    r = run_bass_kernel_spmd(nc, [arrays], core_ids=[0])
    return r.results[0]["result"].reshape(B, S, D)
```
